# Optimizing a Trainium2 kernel written in Bass

```python
import numpy as np
import jax
import jax.numpy as jnp

def _softmax(x, axis=-1):
    return jax.nn.softmax(x, axis=axis)

def _gelu(x):
    return jax.nn.gelu(x, approximate=True)

def _silu(x):
    return jax.nn.silu(x)

def _sigmoid(x):
    return jax.nn.sigmoid(x)

def _layernorm(x, axis=-1, eps=1e-05):
    m = jnp.mean(x, axis=axis, keepdims=True)
    v = jnp.var(x, axis=axis, keepdims=True)
    return (x - m) / jnp.sqrt(v + eps)

def _scatter_add(tgt, idx, src, axis=0):
    return tgt.at[idx].add(src)

def _segment_sum(src, seg, n):
    return jax.ops.segment_sum(src, seg, n)
kernel_name = 'mk_gnn_preln_d1_gnn_r8_3820fc'

def setup_inputs(seed: int=0):
    np.random.seed(seed)
    _w = jnp.asarray

    def _rec_inputs():
        import jax
        import jax.numpy as jnp
        _gk = jax.random.key(seed)
        x = -0.0005121 + 1.001 * jax.random.normal(jax.random.fold_in(_gk, 1), (6250, 64), jnp.float32)
        _s = jax.random.randint(jax.random.fold_in(_gk, 2), (100000,), 0, 6250, jnp.int32)
        _d = jax.random.randint(jax.random.fold_in(_gk, 3), (100000,), 0, 6250, jnp.int32)
        _loop = jnp.arange(6250, dtype=jnp.int32)
        src = jnp.concatenate([_s, _d, _loop])
        dst = jnp.concatenate([_d, _s, _loop])
        _o = jnp.argsort(dst, stable=True)
        src = src[_o]
        dst = dst[_o]
        edge_attr_4 = -0.0005303 + 1.00001 * jax.random.normal(jax.random.fold_in(_gk, 12), (206250, 4), jnp.float32)
        return (x, src, dst, edge_attr_4)
    x, src, dst, edge_attr_4 = _rec_inputs()

    def _L0_gnn_setup():
        import jax, jax.numpy as jnp
        import numpy as np
        import math
        N_NODES = 6250
        N_EDGES = 62500
        HIDDEN = 64
        N_LAYERS = 4
        DELTA = 2.5
        N_AGG = 6
        N_SCALE = 3
        EPS_BN = 1e-05

        def _batchnorm(x, gamma, beta):
            mu = jnp.mean(x, axis=0)
            var = jnp.mean(jnp.square(x - mu), axis=0)
            return (x - mu) * jax.lax.rsqrt(var + EPS_BN) * gamma + beta

        def _pna_layer(h, src, dst, WM, bM, WU, bU, g_t, b_t, Wmix, bmix, g_o, b_o):
            n = h.shape[0]
            msg = jnp.concatenate([h[src], h[dst]], axis=1) @ WM + bM
            deg = jax.ops.segment_sum(jnp.ones(src.shape[0], h.dtype), dst, num_segments=n)
            denom = jnp.maximum(deg, 1.0)[:, None]
            s = jax.ops.segment_sum(msg, dst, num_segments=n)
            mean = s / denom
            mean_sq = jax.ops.segment_sum(msg * msg, dst, num_segments=n) / denom
            var = jax.nn.relu(mean_sq - mean * mean)
            std = jnp.sqrt(var + 1e-30)
            has = (deg > 0)[:, None]
            mx = jnp.where(has, jax.ops.segment_max(msg, dst, num_segments=n), 0.0)
            mn = jnp.where(has, jax.ops.segment_min(msg, dst, num_segments=n), 0.0)
            agg = jnp.concatenate([mean, mx, mn, std, var, s], axis=1)
            logD = jnp.log(deg + 1.0)[:, None]
            amp = logD / DELTA
            att = jnp.where(logD > 0, DELTA / jnp.where(logD > 0, logD, 1.0), 0.0)
            h_neigh = jnp.concatenate([agg, agg * amp, agg * att], axis=1)
            hu = jnp.concatenate([h, h_neigh], axis=1) @ WU + bU
            hu = hu * (1.0 / math.sqrt(n))
            hbn = _batchnorm(hu, g_t, b_t)
            hm = jax.nn.leaky_relu(hbn @ Wmix + bmix, 0.01)
            out = hm + h
            return jax.nn.relu(_batchnorm(out, g_o, b_o)) + h
        key = jax.random.key(seed)
        ks = jax.random.split(key, 12)
        d = HIDDEN
        L = N_LAYERS
        din_u = (N_AGG * N_SCALE + 1) * d
        return {'node_feat': jax.random.normal(ks[0], (N_NODES, d), jnp.float32), 'edge_feat': jax.random.normal(ks[1], (N_EDGES, 4), jnp.float32), 'edge_src': jax.random.randint(ks[2], (N_EDGES,), 0, N_NODES, jnp.int32), 'edge_dst': jax.random.randint(ks[3], (N_EDGES,), 0, N_NODES, jnp.int32), 'WM': jax.random.normal(ks[4], (L, 2 * d, d), jnp.float32) / math.sqrt(2 * d), 'bM': jnp.zeros((L, d), jnp.float32), 'WU': jax.random.normal(ks[5], (L, din_u, d), jnp.float32) / math.sqrt(din_u), 'bU': jnp.zeros((L, d), jnp.float32), 'gamma_t': jnp.ones((L, d), jnp.float32), 'beta_t': jnp.zeros((L, d), jnp.float32), 'Wmix': jax.random.normal(ks[6], (L, d, d), jnp.float32) / math.sqrt(d), 'bmix': jnp.zeros((L, d), jnp.float32), 'gamma_o': jnp.ones((L, d), jnp.float32), 'beta_o': jnp.zeros((L, d), jnp.float32)}
    _L0_gnn_all = _L0_gnn_setup()
    _L0_gnn_in = {k: v for k, v in _L0_gnn_all.items() if k in ('WM', 'bM', 'WU', 'bU', 'gamma_t', 'beta_t', 'Wmix', 'bmix', 'gamma_o', 'beta_o')}
    del _L0_gnn_all
    return {'x': x, 'src': src, 'dst': dst, 'edge_attr_4': edge_attr_4, 'L0_gnn_WM': _L0_gnn_in['WM'], 'L0_gnn_bM': _L0_gnn_in['bM'], 'L0_gnn_WU': _L0_gnn_in['WU'], 'L0_gnn_bU': _L0_gnn_in['bU'], 'L0_gnn_gamma_t': _L0_gnn_in['gamma_t'], 'L0_gnn_beta_t': _L0_gnn_in['beta_t'], 'L0_gnn_Wmix': _L0_gnn_in['Wmix'], 'L0_gnn_bmix': _L0_gnn_in['bmix'], 'L0_gnn_gamma_o': _L0_gnn_in['gamma_o'], 'L0_gnn_beta_o': _L0_gnn_in['beta_o']}

def reference(x, src, dst, edge_attr_4, L0_gnn_WM, L0_gnn_bM, L0_gnn_WU, L0_gnn_bU, L0_gnn_gamma_t, L0_gnn_beta_t, L0_gnn_Wmix, L0_gnn_bmix, L0_gnn_gamma_o, L0_gnn_beta_o):
    import jax
    import jax.numpy as jnp

    def _L0_gnn_ref(node_feat, edge_feat, edge_src, edge_dst, WM, bM, WU, bU, gamma_t, beta_t, Wmix, bmix, gamma_o, beta_o):
        import jax, jax.numpy as jnp
        import numpy as np
        import math
        N_NODES = 6250
        N_EDGES = 62500
        HIDDEN = 64
        N_LAYERS = 4
        DELTA = 2.5
        N_AGG = 6
        N_SCALE = 3
        EPS_BN = 1e-05

        def _batchnorm(x, gamma, beta):
            mu = jnp.mean(x, axis=0)
            var = jnp.mean(jnp.square(x - mu), axis=0)
            return (x - mu) * jax.lax.rsqrt(var + EPS_BN) * gamma + beta

        def _pna_layer(h, src, dst, WM, bM, WU, bU, g_t, b_t, Wmix, bmix, g_o, b_o):
            n = h.shape[0]
            msg = jnp.concatenate([h[src], h[dst]], axis=1) @ WM + bM
            deg = jax.ops.segment_sum(jnp.ones(src.shape[0], h.dtype), dst, num_segments=n)
            denom = jnp.maximum(deg, 1.0)[:, None]
            s = jax.ops.segment_sum(msg, dst, num_segments=n)
            mean = s / denom
            mean_sq = jax.ops.segment_sum(msg * msg, dst, num_segments=n) / denom
            var = jax.nn.relu(mean_sq - mean * mean)
            std = jnp.sqrt(var + 1e-30)
            has = (deg > 0)[:, None]
            mx = jnp.where(has, jax.ops.segment_max(msg, dst, num_segments=n), 0.0)
            mn = jnp.where(has, jax.ops.segment_min(msg, dst, num_segments=n), 0.0)
            agg = jnp.concatenate([mean, mx, mn, std, var, s], axis=1)
            logD = jnp.log(deg + 1.0)[:, None]
            amp = logD / DELTA
            att = jnp.where(logD > 0, DELTA / jnp.where(logD > 0, logD, 1.0), 0.0)
            h_neigh = jnp.concatenate([agg, agg * amp, agg * att], axis=1)
            hu = jnp.concatenate([h, h_neigh], axis=1) @ WU + bU
            hu = hu * (1.0 / math.sqrt(n))
            hbn = _batchnorm(hu, g_t, b_t)
            hm = jax.nn.leaky_relu(hbn @ Wmix + bmix, 0.01)
            out = hm + h
            return jax.nn.relu(_batchnorm(out, g_o, b_o)) + h
        del edge_feat
        h = node_feat
        for i in range(N_LAYERS):
            h = _pna_layer(h, edge_src, edge_dst, WM[i], bM[i], WU[i], bU[i], gamma_t[i], beta_t[i], Wmix[i], bmix[i], gamma_o[i], beta_o[i])
        return h
    h = jnp.maximum(_layernorm(x, axis=-1), 0.0)
    x = x + _L0_gnn_ref(h, edge_attr_4, src, dst, L0_gnn_WM, L0_gnn_bM, L0_gnn_WU, L0_gnn_bU, L0_gnn_gamma_t, L0_gnn_beta_t, L0_gnn_Wmix, L0_gnn_bmix, L0_gnn_gamma_o, L0_gnn_beta_o)
    return x

_drawn_inputs = setup_inputs


def setup_inputs(seed=0):
    import zlib

    import numpy as np

    out = dict(_drawn_inputs(seed))
    spreads = {'L0_gnn_bM': (0.0, 0.453),
     'L0_gnn_bU': (0.0, 0.8),
     'L0_gnn_gamma_t': (1.0, 0.2),
     'L0_gnn_beta_t': (0.0, 0.362),
     'L0_gnn_bmix': (0.0, 0.317),
     'L0_gnn_gamma_o': (1.0, 0.2),
     'L0_gnn_beta_o': (0.0, 0.1)}
    factors = {}
    for name, (base, spread) in spreads.items():
        noise = np.random.default_rng([zlib.crc32(name.encode()), seed]).standard_normal(out[name].shape)
        drawn = base * np.exp(spread * noise) if base else spread * noise
        out[name] = jnp.asarray(drawn.astype(out[name].dtype))
    for name, factor in factors.items():
        out[name] = (out[name] * factor).astype(out[name].dtype)
    return out
```

```python
import math
from contextlib import ExitStack

import concourse.bass as bass
from concourse import mybir

F32, I32, BF16 = mybir.dt.float32, mybir.dt.int32, mybir.dt.bfloat16
ALU = mybir.AluOpType
ACT = mybir.ActivationFunctionType
AX = mybir.AxisListType
ds = bass.ds

P = 128
N = 6250
E = 206250
D = 64
LAYERS = 4
AGGS = 6
DELTA = 2.5
EPS = 1e-5
TILES = -(-N // P)
TT = TILES + 1
HALF = TT // 2
DUMMY = TILES
LAST = N - (TILES - 1) * P
FC = HALF * P
VALID = ((HALF - 1) * P + LAST, (HALF - 1) * P)

BLOCK = 512
BLOCKS = -(-E // BLOCK)
SEARCHES = TILES + 1
LOAD_P = 75
LOAD_F = E // LOAD_P

ROUND = 64
WIN_STEP, WIN = 16, ROUND + 16
WINDOWS = E // WIN_STEP + 1
WIN_DIRECT = (E - WIN) // WIN_STEP + 1
TAIL0 = WIN_DIRECT * WIN_STEP
TAIL_REAL = E - TAIL0
TAIL = (WINDOWS - WIN_DIRECT - 1) * WIN_STEP + WIN

GROUP, SLOTS = 7, 4
BODY = GROUP * SLOTS
ITERS = -(-(ROUND + -(-E // P)) // BODY)
COLS = ITERS * BODY
FLATC = COLS + ROUND
BIG_TILES = -(-(E // (ROUND + 1)) // P)
BIG_GROUP = 4
BINS = ROUND + 2
BT = BINS * TILES
SCAN_CHUNKS = 7
SCAN = BT // SCAN_CHUNKS
PAY = D + 4
HUGE = 3.0e38
MIX = 320
MIXES = FC // MIX

A_AB, A_U, A_U0, A_MIX, A_BM, A_COL = 0, 128, 704, 768, 832, 960
A_ALL = A_COL + 5
W_AB, W_U, W_U0, W_MIX, W_BM, W_BU, W_COL = 0, 256, 832, 960, 1088, 1152, 1216
W_ALL = W_COL + 5
C_BMIX, C_GT, C_BT, C_GO, C_BO = (W_COL + i for i in range(5))
PAIRS = [(5, 4), (1, 2), (0, 3)]


def build(nc, x, src, dst, WM, bM, WU, bU, gamma_t, beta_t, Wmix, bmix, gamma_o, beta_o, out):
    assert BT == SCAN * SCAN_CHUNKS and SCAN <= 512 and FC == MIXES * MIX
    dst_f = nc.dram_tensor("dst_f", (BLOCKS, BLOCK), F32).ap()
    windows = nc.dram_tensor("windows", (WINDOWS, WIN), I32).ap()
    pos_d = nc.dram_tensor("pos_d", (TILES * P, PAY), F32).ap()
    table = nc.dram_tensor("table", (TILES * P, 2 * D), F32).ap()

    with ExitStack() as ctx:
        def sb(name, shape, dt=F32):
            return ctx.enter_context(nc.sbuf_tensor(name, shape, dt))

        def sem(name):
            return ctx.enter_context(nc.semaphore(name))

        onesf = sb("onesf", [P, SCAN])
        ident = sb("ident", [P, P])
        fold = sb("fold", [P, P])
        ones_bf = sb("ones_bf", [P, P], BF16)
        below_bf = sb("below_bf", [P, P], BF16)
        prefix = sb("prefix", [64, TT])
        tiny = sb("tiny", [P, 1])
        epsc = sb("epsc", [P, 1])
        weights = sb("weights", [P, LAYERS, A_ALL])
        W = sb("W", [P, W_ALL])

        flat = sb("flat", [P, 2, FLATC], I32)
        toff = sb("toff", [1, FLATC], I32)
        colo = sb("colo", [1, TT], I32)
        nid = sb("nid", [P, TILES], I32)
        rank_i = sb("rank_i", [P, TILES], I32)
        scal = sb("scal", [P, 8, TT])
        DEG, RDEN, HAS, AMP, ATT, TMP0, TMP1, LEN = (scal[:, k, :] for k in range(8))
        XP = sb("XP", [P, TILES, PAY])

        SS = sb("SS", [P, TT, 2 * D])
        MM = sb("MM", [P, TT, 2 * D])
        MS = sb("MS", [P, TT, 2 * D])
        B = sb("B", [P, TT, D])
        hT = sb("hT", [P, FC])
        HU = sb("HU", [P, TT, D])
        HUT = sb("HUT", [P, FC])
        rows = sb("rows", [P, BODY, 2 * D])
        idx = sb("idx", [P, BODY], I32)
        AGT = sb("AGT", [P, 2, 3 * P])
        UA = sb("UA", [P, 2, D])
        UB = sb("UB", [P, 2, D])
        col = sb("col", [P, 16])
        Z = MS[:, :, :].rearrange("p t f -> p (t f)")[:, 0:FC]
        OT = MS[:, :, :].rearrange("p t f -> p (t f)")[:, FC:2 * FC]
        JUNK = HU[:, :, :].rearrange("p t f -> p (t f)")
        bank = [ctx.enter_context(nc.psum_tensor(f"bank{i}", [P, 512], F32)) for i in range(8)]

        extra = sb("extra", [1, 1], I32)
        kb = sb("kb", [P, 1])
        nd = sb("nd", [P, SEARCHES])
        ndi = sb("ndi", [P, SEARCHES], I32)
        c1 = sb("c1", [P, SEARCHES])
        c2 = sb("c2", [P, SEARCHES])
        blki = sb("blki", [P, SEARCHES], I32)
        rp = sb("rp", [P, SEARCHES])
        key = sb("key", [P, TILES])
        binsi = sb("binsi", [P, ROUND + 2], I32)
        binsf = sb("binsf", [P, ROUND + 2])
        LT = sb("LT", [64, 1])
        LT2 = sb("LT2", [P, 1])
        start_i = sb("start_i", [P, TILES], I32)
        win_i = sb("win_i", [P, TILES], I32)
        offb = sb("offb", [P, 4, TILES], I32)
        flatSS = SS[:, :, :].rearrange("p t f -> p (t f)")
        flatMM = MM[:, :, :].rearrange("p t f -> p (t f)")
        flatHU = HU[:, :, :].rearrange("p t f -> p (t f)")
        big = [flatHU[:, k * WIN:(k + 1) * WIN].bitcast(I32) for k in range(2)]
        big_past = flatHU[:, 2 * WIN:2 * WIN + ROUND].bitcast(I32)
        big_keep = flatHU[:, 2 * WIN + ROUND:2 * WIN + 2 * ROUND]
        b0 = 2 * WIN + 2 * ROUND
        big_start = flatHU[:, b0:b0 + 1]
        big_len = flatHU[:, b0 + 1:b0 + 2]
        big_i, big_win = (flatHU[:, b0 + k:b0 + k + 1].bitcast(I32) for k in (2, 3))
        big_off = flatHU[:, b0 + 4:b0 + 8].bitcast(I32)
        big_idx = flatHU[:, b0 + 8:b0 + 8 + BIG_GROUP].bitcast(I32)
        flatMS = MS[:, :, :].rearrange("p t f -> p (t f)")
        dst_i = flatSS[0:LOAD_P, 0:LOAD_F].bitcast(I32)
        dst_s = flatSS[0:LOAD_P, LOAD_F:2 * LOAD_F]
        samples_i = flatHU[0:1, 0:BLOCKS].bitcast(I32)
        samples = flatHU[0:1, BLOCKS:2 * BLOCKS]
        pad_row = sb("pad_row", [1, BLOCKS * BLOCK - E])
        tail_i = sb("tail_i", [1, TAIL], I32)
        pay = flatMM[:, 0:TILES * PAY].rearrange("p (t f) -> p t f", f=PAY)
        found = flatMS[:, 0:7 * BLOCK].rearrange("p (s b) -> p s b", b=BLOCK)
        junk = flatMS[:, 7 * BLOCK:8 * BLOCK]
        shrug = B[:, :, :].rearrange("p t f -> p (t f)")[:, 0:10 * BLOCK // 2].bitcast(BF16).rearrange("p (s b) -> p s b", b=BLOCK)
        onehot = flatMS[:, 4096:4096 + BT // 2].bitcast(BF16)
        before = flatSS[:, 0:BT]
        winA = flatSS[:, 0:TILES * WIN].bitcast(I32).rearrange("p (t w) -> p t w", w=WIN)
        winB = flatMS[:, 0:TILES * WIN].bitcast(I32).rearrange("p (t w) -> p t w", w=WIN)
        pack = flatMM[:, 0:TILES * 2 * ROUND].bitcast(I32).rearrange("p (t k j) -> p t k j", k=2, j=ROUND)
        past = HU[:, 0:TILES, :].bitcast(I32)
        tvals = hT[0:1, 0:TILES * ROUND].bitcast(I32).rearrange("p (t j) -> p t j", j=ROUND)
        bT = rows[:, :, :].rearrange("p c f -> p (c f)")[:, 0:BT]

        names = ("passed big_reset big_mx big_mx2 big_ready big_found big_rows kb_done big_v big_next big_added ld_x ld_w ld_dst ld_smp dstf_done dstf_st pad_st smp_done smp_ps c1_done win_st tail_ld "
                 "pool_c dve_c c2_done hot_done ps1 ps1_used ps2 rank_done pos_ld win_ld lenT lt_done colps colo_done "
                 "pack_done flat_done toff_done cls pay_done sc_pos xp_act h0_done h0_ps h0_ev v a "
                 "w_now tp tp_used tab_ready tab_sc idx_ready added sums_reset agg_ready agg_half std_done "
                 "tr tr_ev ou ou_used hu_done hut_ps hut_ev st_done fold_ps aff1 hbn_done mix_ps z_done out_done sq_done aff2 r_done h_next "
                 "root fin_ps fin_ev fin_sc").split()
        S = {n: sem(n) for n in names}
        gat = [sem(f"gathered{i}") for i in range(SLOTS)]
        blk_s = [sem(f"block_found{i}") for i in range(7)]

        def wait(eng, s, value):
            eng.wait_ge(S[s] if isinstance(s, str) else s, value)
            if not isinstance(value, int):
                eng.sem_inc(S["passed"])

        def chained(eng, name):
            n = [0]

            def step(ins):
                n[0] += 1
                ins.then_inc(S[name], 1)
                eng.wait_ge(S[name], n[0])
            return step

        prep = nc.Block()
        block = prep.__enter__()

        @block.sync
        def _(sp):
            sp.dma_start(dst_i, dst.rearrange("(p f) -> p f", p=LOAD_P)).then_inc(S["ld_dst"], 16)
            with nc.allow_non_contiguous_dma(reason="one sample of each block"):
                sp.dma_start(samples_i[0:1, :], bass.AP(dst.tensor, 0, [[E, 1], [BLOCK, BLOCKS]])).then_inc(S["ld_smp"], 16)
            sp.wait_ge(S["dve_c"], 1)
            full = N // TILES
            sp.dma_start(pay[0:full, :, 0:D], x[0:full * TILES, :].rearrange("(p i) f -> p i f", i=TILES)).then_inc(S["ld_x"], 16)
            rest = N - full * TILES
            sp.dma_start(pay[full:full + 1, 0:rest, 0:D], x[full * TILES:N, :].rearrange("(p i) f -> p i f", p=1)).then_inc(S["ld_x"], 16)
            even = WIN_DIRECT // 16 * 16
            sp.dma_start(windows[0:even, :], bass.AP(src.tensor, 0, [[WIN_STEP, even], [1, WIN]])).then_inc(S["win_st"], 16)
            sp.dma_start(windows[even:WIN_DIRECT, :],
                         bass.AP(src.tensor, even * WIN_STEP, [[WIN_STEP, WIN_DIRECT - even], [1, WIN]])).then_inc(S["win_st"], 16)
            sp.dma_start(tail_i[0:1, 0:TAIL_REAL], src[TAIL0:E].rearrange("(p f) -> p f", p=1)).then_inc(S["tail_ld"], 16)
            sp.wait_ge(S["tail_ld"], 16)
            for i in range(WINDOWS - WIN_DIRECT):
                sp.dma_start(windows[WIN_DIRECT + i:WIN_DIRECT + i + 1, :],
                             tail_i[0:1, i * WIN_STEP:i * WIN_STEP + WIN]).then_inc(S["win_st"], 16)
            sp.wait_ge(S["dstf_done"], 1)
            sp.dma_start(bass.AP(dst_f.tensor, 0, [[LOAD_F, LOAD_P], [1, LOAD_F]]), dst_s).then_inc(S["dstf_st"], 16)
            sp.dma_start(bass.AP(dst_f.tensor, E, [[BLOCKS * BLOCK - E, 1], [1, BLOCKS * BLOCK - E]]), pad_row[0:1, :]).then_inc(S["dstf_st"], 16)
            sp.wait_ge(S["sc_pos"], 16 * TILES)
            sp.dma_start(XP[:, :, :], pos_d.rearrange("(t p) f -> p t f", p=P)).then_inc(S["pos_ld"], 16)

        @block.scalar
        def _(act):
            act.wait_ge(S["dve_c"], 1)
            for h in range(2):
                r = slice(64 * h, 64 * h + 64)
                w = weights[r, :, :]
                act.dma_start(w[:, :, A_AB:A_AB + 64], WM[:, 0:64, :].rearrange("l k n -> k l n")).then_inc(S["ld_w"], 16)
                act.dma_start(w[:, :, A_AB + 64:A_AB + 128], WM[:, 64:128, :].rearrange("l k n -> k l n")).then_inc(S["ld_w"], 16)
                act.dma_start(w[:, :, A_U0:A_U0 + 64], WU[:, 0:64, :].rearrange("l k n -> k l n")).then_inc(S["ld_w"], 16)
                act.dma_start(w[:, :, A_MIX:A_MIX + 64], Wmix.rearrange("l k n -> k l n")).then_inc(S["ld_w"], 16)
                for c, pair in enumerate(PAIRS):
                    for s in range(3):
                        k0 = 64 + s * AGGS * D + pair[h] * D
                        o = A_U + c * 192 + s * 64
                        act.dma_start(w[:, :, o:o + 64], WU[:, k0:k0 + D, :].rearrange("l k n -> k l n")).then_inc(S["ld_w"], 16)
                with nc.allow_non_contiguous_dma(reason="one value per partition"):
                    for o, v in ((C_BMIX, bmix), (C_GT, gamma_t), (C_BT, beta_t), (C_GO, gamma_o), (C_BO, beta_o)):
                        act.dma_start(w[:, :, A_COL - W_COL + o:A_COL - W_COL + o + 1], v.rearrange("l (k n) -> k l n", n=1)).then_inc(S["ld_w"], 16)
            for o, v in ((A_BM, bM), (A_BM + D, bU)):
                act.dma_start(weights[:, :, o:o + 64], bass.AP(v.tensor, 0, [[0, P], [D, LAYERS], [1, D]])).then_inc(S["ld_w"], 16)
            act.wait_ge(S["win_ld"], 1)
            nc.scalar.activation(TMP1, DEG, ACT.Ln, bias=onesf[:, 0:1]).then_inc(S["a"], 1)
            act.wait_ge(S["pack_done"], 1)
            act.wait_ge(S["colo_done"], 1)
            with act.Fori(0, TILES) as t:
                o = act.value_load(colo[0:1, ds(t, 1)], min_val=0, max_val=COLS)
                wait(act, "flat_done", t + 1)
                nc.scalar.copy(flat[:, :, ds(o, ROUND)],
                               pack[:, ds(t, 1), :, :].rearrange("p t k j -> p (t k) j")).then_inc(S["flat_done"], 1)
            act.wait_ge(S["h0_done"], 1)
            nc.scalar.activation(TMP0, TMP0, ACT.Sqrt).then_inc(S["a"], 1)

        @block.gpsimd
        def _(pool):
            nc.gpsimd.iota(ndi[:, :], pattern=[[1, SEARCHES]], base=0, channel_multiplier=TILES).then_inc(S["pool_c"], 1)
            nc.gpsimd.iota(binsi[:, :], pattern=[[1, BINS]], base=0, channel_multiplier=0).then_inc(S["pool_c"], 1)
            nc.gpsimd.iota(tvals[0:1, :, :], pattern=[[2 * D, TILES], [0, ROUND]], base=0, channel_multiplier=0).then_inc(S["pool_c"], 1)
            pool.wait_ge(S["dve_c"], 1)
            nc.gpsimd.affine_select(out=ident[:, :], in_=onesf[:, 0:P], compare_op=ALU.is_equal, fill=0.0, base=0,
                                    pattern=[[-1, P]], channel_multiplier=1).then_inc(S["pool_c"], 1)
            nc.gpsimd.affine_select(out=junk[:, 0:P], in_=onesf[:, 0:P], compare_op=ALU.is_ge, fill=0.0, base=0,
                                    pattern=[[-1, P]], channel_multiplier=1).then_inc(S["pool_c"], 1)
            nc.gpsimd.affine_select(out=prefix[:, :], in_=onesf[0:64, 0:TT], compare_op=ALU.is_ge, fill=0.0, base=-1,
                                    pattern=[[1, TT]], channel_multiplier=-1).then_inc(S["pool_c"], 1)
            pool.wait_ge(S["dstf_st"], 32)
            for i in range(SEARCHES):
                if i % 10 == 0:
                    pool.wait_ge(S["c1_done"], i // 10 + 1)
                if i >= 7:
                    pool.wait_ge(S["c2_done"], i - 6)
                nc.gpsimd.indirect_dma_start(found[:, i % 7, :], None, dst_f,
                                             bass.IndirectOffsetOnAxis(ap=blki[:, i:i + 1], axis=0)).then_inc(blk_s[i % 7], 16)
            pool.wait_ge(S["rank_done"], 1)
            pool.wait_ge(S["ld_x"], 32)
            for i in range(TILES):
                nc.gpsimd.indirect_dma_start(pos_d, bass.IndirectOffsetOnAxis(ap=rank_i[:, i:i + 1], axis=0),
                                             pay[:, i, :], None).then_inc(S["sc_pos"], 16)
            pool.wait_ge(S["win_ld"], 1)
            pool.wait_ge(S["win_st"], 16 * (2 + WINDOWS - WIN_DIRECT))
            for t in range(TILES):
                nc.gpsimd.indirect_dma_start(winA[:, t, :], None, windows,
                                             bass.IndirectOffsetOnAxis(ap=win_i[:, t:t + 1], axis=0)).then_inc(blk_s[t // 7], 16)

        @block.vector
        def _(dve):
            step = chained(dve, "v")
            nc.vector.memset(onesf[:, :], 1.0)
            nc.vector.memset(ones_bf[:, :], 1.0)
            nc.vector.memset(tiny[:, :], 1e-30)
            nc.vector.memset(epsc[:, :], EPS)
            nc.vector.memset(pad_row[0:1, :], 1.0e9)
            nc.vector.memset(tail_i[0:1, :], 0)
            nc.vector.memset(W[:, :], 0.0)
            nc.vector.memset(scal[:, :, :], 0.0)
            nc.vector.memset(flat[:, :, :], 0)
            nc.vector.memset(toff[0:1, :], DUMMY * 2 * D)
            nc.vector.memset(pay[96:128, :, :], 0.0).then_inc(S["dve_c"], 1)
            dve.wait_ge(S["dve_c"], 1)
            nc.vector.nop().then_inc(S["flat_done"], 1)
            nc.vector.nop().then_inc(S["toff_done"], 1)
            nc.vector.nop().then_inc(S["big_added"], 1)
            nc.vector.nop().then_inc(S["added"], BODY)
            dve.wait_ge(S["ld_smp"], 16)
            nc.vector.tensor_copy(samples[0:1, :], samples_i[0:1, :]).then_inc(S["smp_done"], 1)
            dve.wait_ge(S["ld_dst"], 16)
            nc.vector.tensor_copy(dst_s, dst_i).then_inc(S["dstf_done"], 1)
            dve.wait_ge(S["pool_c"], 6)
            nc.vector.tensor_copy(binsf[:, :], binsi[:, :])
            nc.vector.tensor_scalar(below_bf[:, :], junk[:, 0:P], -1.0, None, ALU.mult)
            step(nc.vector.tensor_copy(nd[:, :], ndi[:, :]))
            nc.vector.tensor_copy(fold[:, 0:64], ident[:, 0:64])
            step(nc.vector.tensor_copy(fold[:, 64:128], ident[:, 64:128]))
            nc.vector.tensor_tensor(fold[:, 0:64], ident[:, 0:64], ident[:, 64:128], ALU.add)
            step(nc.vector.tensor_tensor(fold[:, 64:128], ident[:, 0:64], ident[:, 64:128], ALU.add))
            dve.wait_ge(S["smp_ps"], 1)
            for i in range(SEARCHES):
                ins = nc.vector.tensor_scalar(shrug[:, i % 10, 0:BLOCKS], bank[7][:, 0:BLOCKS], nd[:, i:i + 1], 0.0,
                                              ALU.is_lt, ALU.add, accum_out=c1[:, i:i + 1])
                if i % 10 == 9:
                    step(ins)
                    r = slice(i - 9, i + 1)
                    step(nc.vector.tensor_scalar(c1[:, r], c1[:, r], -1.0, 0.0, ALU.add, ALU.max))
                    nc.vector.tensor_copy(blki[:, r], c1[:, r]).then_inc(S["c1_done"], 1)
            for i in range(SEARCHES):
                dve.wait_ge(blk_s[i % 7], 16 * (i // 7 + 1))
                if i >= 10:
                    dve.wait_ge(S["c2_done"], i - 9)
                nc.vector.tensor_scalar(shrug[:, i % 10, :], found[:, i % 7, :], nd[:, i:i + 1], 0.0,
                                        ALU.is_lt, ALU.add, accum_out=c2[:, i:i + 1]).then_inc(S["c2_done"], 1)
            dve.wait_ge(S["c2_done"], SEARCHES)
            step(nc.vector.scalar_tensor_tensor(rp[:, :], c1[:, :], float(BLOCK), c2[:, :], ALU.mult, ALU.add))
            dve.wait_ge(S["ld_x"], 32)
            payc = pay.rearrange("p t f -> p f t")
            step(nc.vector.tensor_tensor(payc[:, D + 2, :], rp[:, 1:SEARCHES], rp[:, 0:TILES], ALU.subtract))
            nc.vector.tensor_copy(payc[:, D, :], nd[:, 0:TILES])
            nc.vector.tensor_copy(payc[:, D + 1, :], rp[:, 0:TILES])
            nc.vector.memset(payc[:, D + 3, :], 0.0)
            step(nc.vector.tensor_scalar(key[:, :], payc[:, D + 2, :], float(ROUND), -1.0, ALU.min, ALU.mult))
            step(nc.vector.tensor_scalar(c1[:, 0:TILES], nd[:, 0:TILES], float(N), float(ROUND), ALU.is_ge, ALU.add))
            step(nc.vector.tensor_tensor(key[:, :], key[:, :], c1[:, 0:TILES], ALU.add))
            hot = onehot.rearrange("p (c i) -> p c i", i=TILES)
            nc.vector.tensor_tensor(hot, key[:, :].unsqueeze(1).to_broadcast([P, BINS, TILES]),
                                    binsf[:, :].unsqueeze(2).to_broadcast([P, BINS, TILES]), ALU.is_equal).then_inc(S["hot_done"], 1)
            for k in range(SCAN_CHUNKS):
                dve.wait_ge(S["ps1"], k + 1)
                r = slice(k * SCAN, (k + 1) * SCAN)
                step(nc.vector.tensor_tensor_scan(before[:, r], onesf[:, 0:SCAN], bank[k][:, 0:SCAN],
                                                  before[:, k * SCAN - 1:k * SCAN] if k else 0.0, ALU.mult, ALU.add))
                nc.vector.nop().then_inc(S["ps1_used"], 1)
            for k in range(SCAN_CHUNKS):
                dve.wait_ge(S["ps2"], k + 1)
                r = slice(k * SCAN, (k + 1) * SCAN)
                step(nc.vector.tensor_tensor(bT[:, r], before[:, r], bank[k][:, 0:SCAN], ALU.add))
            step(nc.vector.tensor_tensor(bT, bT, onehot, ALU.mult))
            step(nc.vector.tensor_reduce(c2[:, 0:TILES], bT.rearrange("p (c i) -> p i c", i=TILES), AX.X, ALU.add))
            nc.vector.tensor_copy(rank_i[:, :], c2[:, 0:TILES]).then_inc(S["rank_done"], 1)

            dve.wait_ge(S["pos_ld"], 16)
            XC = XP[:, :, :].rearrange("p t f -> p f t")
            nc.vector.tensor_copy(nid[:, :], XC[:, D, :])
            nc.vector.tensor_copy(DEG[:, 0:TILES], XC[:, D + 2, :])
            step(nc.vector.tensor_copy(start_i[:, :], XC[:, D + 1, :]))
            nc.vector.tensor_scalar(LEN, DEG, float(ROUND), None, ALU.min)
            for k in range(4):
                nc.vector.tensor_scalar(offb[:, k, :], start_i[:, :], 8 >> k, None, ALU.bitwise_and)
            step(nc.vector.tensor_scalar(win_i[:, :], start_i[:, :], 4, None, ALU.arith_shift_right))
            nc.vector.nop().then_inc(S["win_ld"], 1)
            dve.wait_ge(S["lenT"], 1)
            step(nc.vector.tensor_reduce(LT[0:TILES, :], bank[0][0:TILES, 0:P], AX.X, ALU.max))
            nc.vector.nop().then_inc(S["lt_done"], 1)
            step(nc.vector.tensor_tensor(past, binsf[:, 0:ROUND].unsqueeze(1).to_broadcast([P, TILES, ROUND]),
                                         LEN[:, 0:TILES].unsqueeze(2).to_broadcast([P, TILES, ROUND]), ALU.is_ge))
            step(nc.vector.tensor_scalar(pack[:, :, 1, :], past, -1.0, 1.0, ALU.mult, ALU.add))
            step(nc.vector.tensor_reduce(LT2[:, :], DEG, AX.X, ALU.max))
            nc.vector.nop().then_inc(S["big_mx"], 1)
            dve.wait_ge(S["big_mx2"], 1)
            step(nc.vector.tensor_reduce(LT2[0:1, :], bank[2][0:1, 0:P], AX.X, ALU.max))
            step(nc.vector.tensor_scalar(extra[0:1, :], LT2[0:1, :], -1.0, 0.0, ALU.add, ALU.max))
            step(nc.vector.tensor_scalar(extra[0:1, :], extra[0:1, :], ROUND.bit_length() - 1, None, ALU.arith_shift_right))
            dve.wait_ge(S["colps"], 1)
            step(nc.vector.tensor_copy(colo[0:1, :], bank[1][0:1, 0:TT]))
            nc.vector.nop().then_inc(S["colo_done"], 1)
            for t in range(TILES):
                if t % 7 == 0:
                    g = t // 7
                    dve.wait_ge(blk_s[g], 16 * (len(range(g, SEARCHES, 7)) + 7))
            cur, nxt, w = winA, winB, WIN
            for k in range(4):
                s = 8 >> k
                w -= s
                step(nc.vector.tensor_copy(nxt[:, :, 0:w], cur[:, :, 0:w]))
                step(nc.vector.copy_predicated(nxt[:, :, 0:w], offb[:, k, :].unsqueeze(2).to_broadcast([P, TILES, w]),
                                               cur[:, :, s:s + w]))
                cur, nxt = nxt, cur
            step(nc.vector.tensor_copy(pack[:, :, 0, :], cur[:, :, 0:ROUND]))
            step(nc.vector.copy_predicated(pack[:, :, 0, :], past, cur[:, :, 0:1].to_broadcast([P, TILES, ROUND])))
            nc.vector.nop().then_inc(S["pack_done"], 1)
            with dve.Fori(0, TILES) as t:
                o = dve.value_load(colo[0:1, ds(t, 1)], min_val=0, max_val=COLS)
                if True:
                    wait(dve, "toff_done", t + 1)
                nc.vector.tensor_copy(toff[0:1, ds(o, ROUND)],
                                      tvals[0:1, ds(t, 1), :].rearrange("p t j -> p (t j)")).then_inc(S["toff_done"], 1)
            nc.vector.tensor_scalar(HAS, DEG, 1.0, None, ALU.min)
            step(nc.vector.tensor_scalar(TMP0, DEG, 1.0, None, ALU.max))
            step(nc.vector.reciprocal(RDEN, TMP0))
            dve.wait_ge(S["a"], 1)
            nc.vector.tensor_scalar(AMP, TMP1, 1.0 / DELTA, None, ALU.mult)
            step(nc.vector.tensor_scalar(TMP0, TMP1, 0.5, None, ALU.max))
            step(nc.vector.reciprocal(TMP0, TMP0))
            step(nc.vector.scalar_tensor_tensor(ATT, TMP0, DELTA, HAS, ALU.mult, ALU.mult))
            x3 = XP[:, :, 0:D]
            h0 = B[:, 0:TILES, :]
            b3 = [P, TILES, D]
            nc.vector.memset(B[:, TILES, :], 0.0)
            step(nc.vector.tensor_reduce(TMP0[:, 0:TILES], x3, AX.X, ALU.add))
            step(nc.vector.tensor_scalar(TMP0, TMP0, 1.0 / D, None, ALU.mult))
            step(nc.vector.tensor_tensor(h0, x3, TMP0[:, 0:TILES].unsqueeze(2).to_broadcast(b3), ALU.subtract))
            step(nc.vector.tensor_tensor(HU[:, 0:TILES, :], h0, h0, ALU.mult))
            step(nc.vector.tensor_reduce(TMP0[:, 0:TILES], HU[:, 0:TILES, :], AX.X, ALU.add))
            step(nc.vector.tensor_scalar(TMP0, TMP0, 1.0 / D, EPS, ALU.mult, ALU.add))
            nc.vector.nop().then_inc(S["h0_done"], 1)
            dve.wait_ge(S["a"], 2)
            step(nc.vector.reciprocal(TMP1, TMP0))
            step(nc.vector.tensor_tensor(h0, h0, TMP1[:, 0:TILES].unsqueeze(2).to_broadcast(b3), ALU.mult))
            step(nc.vector.tensor_scalar(B[:, :, :], B[:, :, :], 0.0, None, ALU.max))
            nc.vector.nop().then_inc(S["h0_done"], 1)
            for j in range(HALF):
                dve.wait_ge(S["h0_ps"], j + 1)
                nc.vector.tensor_copy(hT[:, j * P:(j + 1) * P], bank[2 + j % 2][:, 0:P]).then_inc(S["h0_ev"], 1)

        @block.tensor
        def _(pe):
            pe.wait_ge(S["smp_done"], 1)
            pe.wait_ge(S["dve_c"], 1)
            nc.tensor.matmul(bank[7][:, 0:BLOCKS], onesf[0:1, 0:P], samples[0:1, :], start=True, stop=True).then_inc(S["smp_ps"], 1)
            pe.wait_ge(S["hot_done"], 1)
            for k in range(SCAN_CHUNKS):
                nc.tensor.matmul(bank[k][:, 0:SCAN], ones_bf[:, :], onehot[:, k * SCAN:(k + 1) * SCAN],
                                 start=True, stop=True).then_inc(S["ps1"], 1)
            for k in range(SCAN_CHUNKS):
                pe.wait_ge(S["ps1_used"], k + 1)
                nc.tensor.matmul(bank[k][:, 0:SCAN], below_bf[:, :], onehot[:, k * SCAN:(k + 1) * SCAN],
                                 start=True, stop=True).then_inc(S["ps2"], 1)
            pe.wait_ge(S["win_ld"], 1)
            nc.tensor.transpose(bank[0][0:TILES, 0:P], LEN[:, 0:TILES], ident[:, :]).then_inc(S["lenT"], 1)
            pe.wait_ge(S["lt_done"], 1)
            nc.tensor.matmul(bank[1][0:1, 0:TT], LT[0:TILES, :], prefix[0:TILES, :], start=True, stop=True).then_inc(S["colps"], 1)
            pe.wait_ge(S["big_mx"], 1)
            nc.tensor.transpose(bank[2][0:1, 0:P], LT2[:, :], ident[:, :]).then_inc(S["big_mx2"], 1)
            pe.wait_ge(S["h0_done"], 2)
            for j in range(HALF):
                if j >= 2:
                    pe.wait_ge(S["h0_ev"], j - 1)
                nc.tensor.transpose(bank[2 + j % 2][:, 0:P], B[:, 2 * j:2 * j + 2, :], ident[:, :]).then_inc(S["h0_ps"], 1)
        prep.__exit__(None, None, None)

        block = ctx.enter_context(nc.Block())

        sums = SS[:, :, :].rearrange("p t f -> p (t f)")
        exts = MM[:, :, :].rearrange("p t f -> p (t f)")

        CH = 5
        CHUNKS = TT // CH
        BIG_STEPS = 17
        STEPS_ALL = 1 + 7 * CHUNKS + 2 * TT + 2 * 6 + 2 * MIXES + 5

        def load_offsets(dve, c0):
            _, values = nc.values_load_multi_w_load_instructions(
                toff[0:1, ds(c0, GROUP)], engines=[mybir.EngineType.DVE], min_val=0, max_val=DUMMY * 2 * D,
                skip_runtime_bounds_check_because="toff holds tile numbers up to DUMMY, times 2 * D")
            return values

        h3 = hT[:, :].rearrange("p (j n) -> p j n", n=P)
        HUT3 = HUT[:, :].rearrange("p (j n) -> p j n", n=P)
        XPx = XP[:, :, 0:D]
        c_sum, c_mu, c_sq, c_var, c_std, c_rstd, c_scale, c_bias, c_nmu, c_t = (col[:, k:k + 1] for k in range(10))
        halves = ((slice(0, 64), VALID[0]), (slice(64, 128), VALID[1]))

        @block.sync
        def _(sp):
            sp.wait_ge(S["fin_sc"], 16 * TILES)

        @block.gpsimd
        def _(pool):
            more = pool.value_load(extra[0:1, 0:1], min_val=0, max_val=E // ROUND)
            with pool.Fori(0, LAYERS) as l:
                for t in range(TILES):
                    if t % 2 == 0:
                        wait(pool, "tab_ready", l * HALF + t // 2 + 1)
                    nc.gpsimd.indirect_dma_start(table, bass.IndirectOffsetOnAxis(ap=nid[:, t:t + 1], axis=0),
                                                 MS[:, t, :], None).then_inc(S["tab_sc"], 16)
                wait(pool, "tab_sc", l * (16 * TILES) + 16 * TILES)
                with pool.If(more > 0):
                    with pool.Fori(0, more) as k:
                        with pool.Fori(0, BIG_TILES) as t:
                            n = (l * more + k) * BIG_TILES + t
                            wait(pool, "big_ready", n + 1)
                            nc.gpsimd.indirect_dma_start(big[0], None, windows,
                                                         bass.IndirectOffsetOnAxis(ap=big_win, axis=0)).then_inc(S["big_found"], 16)
                            with pool.Fori(0, ROUND // BIG_GROUP) as q:
                                wait(pool, "big_next", n * (ROUND // BIG_GROUP) + q + 1)
                                for c in range(BIG_GROUP):
                                    nc.gpsimd.indirect_dma_start(rows[:, c, :], None, table,
                                                                 bass.IndirectOffsetOnAxis(ap=big_idx[:, c:c + 1], axis=0)).then_inc(S["big_rows"], 16)
                            wait(pool, "big_added", (n + 1) * ROUND + 1)
                            nc.gpsimd.inc_swdge_sem([S["big_found"], S["big_rows"]], [16, 16 * ROUND], mode="sub")
                            pool.sem_inc(S["big_reset"])
                    pool.sem_inc(S["passed"])
                with pool.Fori(0, ITERS) as i:
                    for b in range(SLOTS):
                        wait(pool, "idx_ready", l * (ITERS * SLOTS) + i * SLOTS + b + 1)
                        for k in range(b * GROUP, (b + 1) * GROUP):
                            nc.gpsimd.indirect_dma_start(rows[:, k, :], None, table,
                                                         bass.IndirectOffsetOnAxis(ap=idx[:, k:k + 1], axis=0)).then_inc(gat[b], 16)
            for t in range(TILES):
                if t % 2 == 0:
                    pool.wait_ge(S["fin_ev"], t // 2 + 1)
                nc.gpsimd.indirect_dma_start(out, bass.IndirectOffsetOnAxis(ap=nid[:, t:t + 1], axis=0),
                                             HU[:, t, :], None, bounds_check=N - 1, oob_is_err=False).then_inc(S["fin_sc"], 16)

        @block.scalar
        def _(act):
            with act.Fori(0, LAYERS) as l:
                for j in range(HALF):
                    wait(act, "tp", l * HALF + j + 1)
                    tp = bank[j % 2][:, 0:2 * D].rearrange("p (a f) -> p a f", a=2)
                    nc.scalar.copy(MS[:, 2 * j:2 * j + 2, 0:D], tp)
                    nc.scalar.activation(MS[:, 2 * j:2 * j + 2, D:2 * D], tp, ACT.Square).then_inc(S["tab_ready"], 1)
                with act.Fori(0, ITERS) as i:
                    for b in range(SLOTS):
                        wait(act, "added", l * COLS + i * BODY + (b + 1) * GROUP)
                        nc.scalar.copy(idx[:, b * GROUP:(b + 1) * GROUP],
                                       flat[:, 0, ds(i * BODY + b * GROUP, GROUP)]).then_inc(S["idx_ready"], 1)
                def roots(c):
                    wait(act, "agg_half", l * CHUNKS + c + 1)
                    nc.scalar.activation(MS[:, c * CH:(c + 1) * CH, D:2 * D], SS[:, c * CH:(c + 1) * CH, D:2 * D],
                                         ACT.Sqrt, bias=tiny[:, :]).then_inc(S["std_done"], 1)
                roots(0)
                for c in range(CHUNKS):
                    if c + 1 < CHUNKS:
                        roots(c + 1)
                    for t in range(c * CH, (c + 1) * CH):
                        wait(act, "tr", l * TT + t + 1)
                        nc.scalar.copy(AGT[:, t % 2, :], bank[2 + t % 2][:, 0:3 * P]).then_inc(S["tr_ev"], 1)
                for j in range(HALF):
                    wait(act, "hut_ps", l * HALF + j + 1)
                    nc.scalar.copy(HUT3[:, j, :], bank[6 + j % 2][:, 0:P]).then_inc(S["hut_ev"], 1)

                def norm(n, src):
                    wait(act, "st_done", l * 6 + 3 * n + 2)
                    for h, (r, v) in enumerate(halves):
                        ins = nc.scalar.activation(JUNK[r, 0:v], src[r, 0:v], ACT.Square, bias=c_nmu[r, :],
                                                   accum_out=c_sq[r, :])
                    ins.then_inc(S["sq_done"], 1)
                    wait(act, "st_done", l * 6 + 3 * n + 3)
                    nc.scalar.activation(c_std, c_var, ACT.Sqrt, bias=epsc[:, :]).then_inc(S["root"], 1)

                norm(0, HUT)
                wait(act, "aff1", l + 1)
                for m in range(MIXES):
                    r = slice(m * MIX, (m + 1) * MIX)
                    nc.scalar.activation(HUT[:, r], HUT[:, r], ACT.Identity, bias=c_bias, scale=c_scale).then_inc(S["hbn_done"], 1)
                for m in range(MIXES):
                    r = slice(m * MIX, (m + 1) * MIX)
                    wait(act, "mix_ps", l * MIXES + m + 1)
                    nc.scalar.activation(Z[:, r], bank[m % 4][:, 0:MIX], ACT.Identity,
                                         bias=W[:, C_BMIX:C_BMIX + 1]).then_inc(S["z_done"], 1)
                norm(1, OT)
                wait(act, "aff2", l + 1)
                for m in range(5):
                    r = slice(m * 640, (m + 1) * 640)
                    nc.scalar.activation(OT[:, r], OT[:, r], ACT.Relu, bias=c_bias, scale=c_scale).then_inc(S["r_done"], 1)

        @block.vector
        def _(dve):
            dve.wait_ge(S["ld_w"], 16 * (2 * (4 + 9 + 5) + 2))

            def further_rounds(l):
                nc.vector.memset(kb[:, :], float(ROUND)).then_inc(S["kb_done"], 1)
                wait(dve, "kb_done", (l * (more + 1)) + 1)
                with dve.Fori(0, more) as k:
                    with dve.Fori(0, BIG_TILES) as t:
                        n = (l * more + k) * BIG_TILES + t
                        count = [0]

                        def step(ins):
                            count[0] += 1
                            ins.then_inc(S["big_v"], 1)
                            wait(dve, "big_v", n * BIG_STEPS + count[0])

                        deg = DEG[:, ds(t, 1)]
                        first = XP[:, ds(t, 1), D + 1:D + 2].rearrange("p t f -> p (t f)")
                        step(nc.vector.tensor_scalar(big_start, deg, -1.0, 0.0, ALU.add, ALU.max))
                        step(nc.vector.tensor_scalar(big_start, big_start, kb[:, :], None, ALU.min))
                        step(nc.vector.tensor_tensor(big_start, big_start, first, ALU.add))
                        step(nc.vector.tensor_scalar(big_len, deg, kb[:, :], None, ALU.subtract))
                        step(nc.vector.tensor_copy(big_i, big_start))
                        for b in range(4):
                            nc.vector.tensor_scalar(big_off[:, b:b + 1], big_i, 8 >> b, None, ALU.bitwise_and)
                        nc.vector.tensor_scalar(big_past, binsf[:, 0:ROUND], big_len, None, ALU.is_ge)
                        step(nc.vector.tensor_scalar(big_win, big_i, 4, None, ALU.arith_shift_right))
                        step(nc.vector.tensor_scalar(big_keep, big_past, -1.0, 1.0, ALU.mult, ALU.add))
                        nc.vector.nop().then_inc(S["big_ready"], 1)
                        dve.wait_ge(S["big_found"], 16)
                        cur, nxt, w = *big, WIN
                        for b in range(4):
                            s = 8 >> b
                            w -= s
                            step(nc.vector.tensor_copy(nxt[:, 0:w], cur[:, 0:w]))
                            step(nc.vector.copy_predicated(nxt[:, 0:w], big_off[:, b:b + 1].to_broadcast([P, w]), cur[:, s:s + w]))
                            cur, nxt = nxt, cur
                        step(nc.vector.tensor_copy(nxt[:, 0:ROUND], cur[:, 0:ROUND]))
                        step(nc.vector.copy_predicated(nxt[:, 0:ROUND], big_past, cur[:, 0:1].to_broadcast([P, ROUND])))
                        assert count[0] == BIG_STEPS, count[0]
                        with dve.Fori(0, ROUND // BIG_GROUP) as q:
                            m = n * (ROUND // BIG_GROUP) + q
                            nc.vector.tensor_copy(big_idx, nxt[:, ds(q * BIG_GROUP, BIG_GROUP)]).then_inc(S["big_next"], 1)
                            wait(dve, "big_rows", q * (16 * BIG_GROUP) + 16 * BIG_GROUP)
                            for c in range(BIG_GROUP):
                                row = rows[:, c, :]
                                wait(dve, "big_added", m * BIG_GROUP + c + 1)
                                nc.vector.scalar_tensor_tensor(sums[:, ds(t * (2 * D), 2 * D)], row, big_keep[:, ds(q * BIG_GROUP + c, 1)],
                                                               sums[:, ds(t * (2 * D), 2 * D)], ALU.mult, ALU.add)
                                nc.vector.tensor_tensor(exts[:, ds(t * (2 * D), D)], exts[:, ds(t * (2 * D), D)], row[:, 0:D], ALU.max)
                                nc.vector.tensor_tensor(exts[:, ds(t * (2 * D) + D, D)], exts[:, ds(t * (2 * D) + D, D)], row[:, 0:D],
                                                        ALU.min).then_inc(S["big_added"], 1)
                        wait(dve, "big_reset", n + 1)
                    nc.vector.tensor_scalar(kb[:, :], kb[:, :], float(ROUND), None, ALU.add).then_inc(S["kb_done"], 1)
                    wait(dve, "kb_done", l * (more + 1) + k + 2)
                wait(dve, "big_added", (l * more + more) * (BIG_TILES * ROUND) + 1)

            more = dve.value_load(extra[0:1, 0:1], min_val=0, max_val=E // ROUND)
            with dve.Fori(0, LAYERS) as l:
                n_step = [0]

                def step(ins):
                    n_step[0] += 1
                    ins.then_inc(S["cls"], 1)
                    wait(dve, "cls", l * STEPS_ALL + n_step[0])

                now = weights[:, ds(l, 1), :].rearrange("p l w -> p (l w)")
                for h in range(2):
                    r = slice(64 * h, 64 * h + 64)
                    for o, a, n in ((W_AB + 64 * h, A_AB, 64), (W_AB + 128 + 64 * h, A_AB + 64, 64), (W_U0 + 64 * h, A_U0, 64), (W_MIX + 64 * h, A_MIX, 64)):
                        nc.vector.tensor_copy(W[r, o:o + n], now[r, a:a + n])
                nc.vector.tensor_copy(W[:, W_U:W_U + 576], now[:, A_U:A_U + 576])
                nc.vector.tensor_copy(W[:, W_BM:W_ALL], now[:, A_BM:A_ALL]).then_inc(S["w_now"], 1)
                wait(dve, "w_now", l + 1)
                for j in range(HALF):
                    wait(dve, "tp", l * HALF + j + 1)
                    tp = bank[2 + j % 2][:, 0:2 * D].rearrange("p (a f) -> p a f", a=2)
                    nc.vector.tensor_tensor(B[:, 2 * j:2 * j + 2, :], tp,
                                            W[:, W_BM:W_BM + D].unsqueeze(1).to_broadcast([P, 2, D]), ALU.add).then_inc(S["tp_used"], 1)
                nc.vector.memset(SS[:, :, :], 0.0)
                nc.vector.memset(MM[:, :, 0:D], -HUGE)
                step(nc.vector.memset(MM[:, :, D:2 * D], HUGE))
                with dve.If(more > 0):
                    further_rounds(l)
                with dve.Fori(0, ITERS) as i:
                    for b in range(SLOTS):
                        c0 = i * BODY + b * GROUP
                        wait(dve, gat[b], (l * ITERS + i) * (16 * GROUP) + 16 * GROUP)
                        offs = load_offsets(dve, c0)
                        for k in range(GROUP):
                            row, o = rows[:, b * GROUP + k, :], offs[k]
                            dve.wait_ge(S["added"], l * COLS + c0 + k + BODY)
                            nc.vector.scalar_tensor_tensor(sums[:, ds(o, 2 * D)], row, flat[:, 1, ds(c0 + k, 1)],
                                                           sums[:, ds(o, 2 * D)], ALU.mult, ALU.add)
                            nc.vector.tensor_tensor(exts[:, ds(o, D)], exts[:, ds(o, D)], row[:, 0:D], ALU.max)
                            ins = nc.vector.tensor_tensor(exts[:, ds(o + D, D)], exts[:, ds(o + D, D)], row[:, 0:D], ALU.min)
                            ins.then_inc(S["added"], 1)
                wait(dve, "added", (l + 1) * COLS + BODY)

                def aggregates(c):
                    r = slice(c * CH, (c + 1) * CH)
                    b3 = [P, CH, D]
                    bc = lambda v: v[:, r].unsqueeze(2).to_broadcast(b3)
                    s, q, mx, mn = SS[:, r, 0:D], SS[:, r, D:], MM[:, r, 0:D], MM[:, r, D:]
                    mean, u, b = MS[:, r, 0:D], HU[:, r, :], B[:, r, :]
                    TTo = nc.vector.tensor_tensor
                    TTo(mean, s, bc(RDEN), ALU.mult)
                    step(TTo(q, q, bc(RDEN), ALU.mult))
                    step(TTo(u, mean, mean, ALU.mult))
                    step(TTo(q, q, u, ALU.subtract))
                    step(nc.vector.tensor_scalar(q, q, 0.0, None, ALU.max))
                    nc.vector.nop().then_inc(S["agg_half"], 1)
                    TTo(mx, mx, b, ALU.add)
                    TTo(mn, mn, b, ALU.add)
                    step(TTo(u, b, bc(DEG), ALU.mult))
                    TTo(s, s, u, ALU.add)
                    TTo(mx, mx, bc(HAS), ALU.mult)
                    TTo(mn, mn, bc(HAS), ALU.mult)
                    step(TTo(b, b, bc(HAS), ALU.mult))
                    step(TTo(mean, mean, b, ALU.add))
                    nc.vector.nop().then_inc(S["agg_ready"], 1)

                def combine(c):
                    for t in range(c * CH, (c + 1) * CH):
                        wait(dve, "ou", l * TT + t + 1)
                        o = bank[4 + t % 2]
                        u, v = UA[:, t % 2, :], UB[:, t % 2, :]
                        step(nc.vector.scalar_tensor_tensor(u, o[:, D:2 * D], AMP[:, t:t + 1], W[:, W_BU:W_BU + D], ALU.mult, ALU.add))
                        step(nc.vector.scalar_tensor_tensor(v, o[:, 2 * D:3 * D], ATT[:, t:t + 1], u, ALU.mult, ALU.add))
                        nc.vector.tensor_tensor(HU[:, t, :], o[:, 0:D], v, ALU.add).then_inc(S["hu_done"], 1)

                aggregates(0)
                for c in range(CHUNKS):
                    if c + 1 < CHUNKS:
                        aggregates(c + 1)
                    combine(c)

                def norm(n, src, scale2, gam, bet):
                    for h, (r, v) in enumerate(halves):
                        ins = nc.vector.tensor_reduce(c_sum[r, :], src[r, 0:v], AX.X, ALU.add)
                    step(ins)
                    nc.vector.nop().then_inc(S["st_done"], 1)
                    wait(dve, "fold_ps", l * 4 + 2 * n + 1)
                    step(nc.vector.tensor_scalar(c_nmu, bank[7][:, 0:1], -1.0 / N, None, ALU.mult))
                    nc.vector.nop().then_inc(S["st_done"], 1)
                    wait(dve, "fold_ps", l * 4 + 2 * n + 2)
                    step(nc.vector.tensor_scalar(c_var, bank[7][:, 0:1], scale2 / N, None, ALU.mult))
                    nc.vector.nop().then_inc(S["st_done"], 1)
                    wait(dve, "root", l * 2 + n + 1)
                    step(nc.vector.reciprocal(c_rstd, c_std))
                    step(nc.vector.tensor_scalar(c_scale, c_rstd, W[:, gam:gam + 1], math.sqrt(scale2), ALU.mult, ALU.mult))
                    step(nc.vector.scalar_tensor_tensor(c_bias, c_nmu, c_scale, W[:, bet:bet + 1], ALU.mult, ALU.add))

                wait(dve, "hut_ev", (l + 1) * HALF)
                norm(0, HUT, 1.0 / N, C_GT, C_BT)
                nc.vector.nop().then_inc(S["aff1"], 1)
                for m in range(MIXES):
                    r = slice(m * MIX, (m + 1) * MIX)
                    wait(dve, "z_done", l * MIXES + m + 1)
                    step(nc.vector.scalar_tensor_tensor(OT[:, r], Z[:, r], 0.01, Z[:, r], ALU.mult, ALU.max))
                    step(nc.vector.tensor_tensor(OT[:, r], OT[:, r], hT[:, r], ALU.add))
                norm(1, OT, 1.0, C_GO, C_BO)
                nc.vector.nop().then_inc(S["aff2"], 1)
                for m in range(5):
                    r = slice(m * 640, (m + 1) * 640)
                    wait(dve, "r_done", l * 5 + m + 1)
                    step(nc.vector.tensor_tensor(hT[:, r], OT[:, r], hT[:, r], ALU.add))
                nc.vector.nop().then_inc(S["h_next"], 1)
                assert n_step[0] == STEPS_ALL, n_step[0]
            for j in range(HALF):
                dve.wait_ge(S["fin_ps"], j + 1)
                n = min(2, TILES - 2 * j)
                nc.vector.tensor_tensor(HU[:, 2 * j:2 * j + n, :], bank[j % 2][:, 0:n * D].rearrange("p (a f) -> p a f", a=n),
                                        XPx[:, 2 * j:2 * j + n, :], ALU.add).then_inc(S["fin_ev"], 1)

        @block.tensor
        def _(pe):
            with pe.Fori(0, LAYERS) as l:
                wait(pe, "w_now", l + 1)
                for j in range(HALF):
                    if j >= 2:
                        wait(pe, "tab_ready", l * HALF + j - 1)
                        wait(pe, "tp_used", l * HALF + j - 1)
                    nc.tensor.matmul(bank[j % 2][:, 0:P], h3[:, j, :], W[:, W_AB:W_AB + P], start=True, stop=True)
                    nc.tensor.matmul(bank[2 + j % 2][:, 0:P], h3[:, j, :], W[:, W_AB + P:W_AB + 2 * P], start=True, stop=True).then_inc(S["tp"], 1)
                def turn(t):
                    wait(pe, "agg_ready", l * CHUNKS + t // CH + 1)
                    wait(pe, "std_done", l * CHUNKS + t // CH + 1)
                    if t >= 2:
                        wait(pe, "tr_ev", l * TT + t - 1)
                    for k, src in enumerate((SS, MM, MS)):
                        ins = nc.tensor.transpose(bank[2 + t % 2][:, k * P:(k + 1) * P], src[:, t, :], ident[:, :])
                    ins.then_inc(S["tr"], 1)

                def update(t):
                    wait(pe, "tr_ev", l * TT + t + 1)
                    if t >= 2:
                        wait(pe, "hu_done", l * TT + t - 1)
                    o = bank[4 + t % 2]
                    u0 = W_U0 + 64 * (t % 2)
                    nc.tensor.matmul(o[:, 0:192], AGT[:, t % 2, 0:P], W[:, W_U:W_U + 192], start=True, stop=False)
                    nc.tensor.matmul(o[:, 0:64], h3[:, t // 2, :], W[:, u0:u0 + 64], start=False, stop=False)
                    nc.tensor.matmul(o[:, 0:192], AGT[:, t % 2, P:2 * P], W[:, W_U + 192:W_U + 384], start=False, stop=False)
                    nc.tensor.matmul(o[:, 0:192], AGT[:, t % 2, 2 * P:3 * P], W[:, W_U + 384:W_U + 576],
                                     start=False, stop=True).then_inc(S["ou"], 1)
                turn(0)
                for t in range(TT):
                    if t + 1 < TT:
                        turn(t + 1)
                    update(t)
                wait(pe, "hu_done", (l + 1) * TT)
                for j in range(HALF):
                    if j >= 2:
                        wait(pe, "hut_ev", l * HALF + j - 1)
                    nc.tensor.transpose(bank[6 + j % 2][:, 0:P], HU[:, 2 * j:2 * j + 2, :], ident[:, :]).then_inc(S["hut_ps"], 1)

                def norm(n):
                    wait(pe, "st_done", l * 6 + 3 * n + 1)
                    nc.tensor.matmul(bank[7][:, 0:1], fold[:, :], c_sum, start=True, stop=True).then_inc(S["fold_ps"], 1)
                    wait(pe, "sq_done", l * 2 + n + 1)
                    nc.tensor.matmul(bank[7][:, 0:1], fold[:, :], c_sq, start=True, stop=True).then_inc(S["fold_ps"], 1)
                norm(0)
                for m in range(MIXES):
                    wait(pe, "hbn_done", l * MIXES + m + 1)
                    if m >= 4:
                        wait(pe, "z_done", l * MIXES + m - 3)
                    nc.tensor.matmul(bank[m % 4][:, 0:MIX], W[:, W_MIX:W_MIX + P], HUT[:, m * MIX:(m + 1) * MIX],
                                     start=True, stop=True).then_inc(S["mix_ps"], 1)
                norm(1)
                wait(pe, "h_next", l + 1)
            for j in range(HALF):
                if j >= 2:
                    pe.wait_ge(S["fin_ev"], j - 1)
                nc.tensor.transpose(bank[j % 2][:, 0:P], h3[:, j, :], ident[:, :]).then_inc(S["fin_ps"], 1)


_INS = ["x", "src", "dst", "WM", "bM", "WU", "bU", "gamma_t", "beta_t", "Wmix", "bmix", "gamma_o", "beta_o"]


def kernel(**inputs):
    import numpy as np
    import concourse.bacc as bacc
    from concourse.bass_utils import run_bass_kernel_spmd

    nc = bacc.Bacc("TRN2", target_bir_lowering=False, num_devices=1)
    arrays, args = {}, []
    for name in _INS:
        a = np.ascontiguousarray(inputs[name if name in ("x", "src", "dst") else "L0_gnn_" + name])
        arrays[f"in_{name}"] = a
        args.append(nc.dram_tensor(f"in_{name}", a.shape, mybir.dt.from_np(a.dtype), kind="ExternalInput").ap())
    out = nc.dram_tensor("out_x", (N, D), F32, kind="ExternalOutput").ap()
    build(nc, *args, out)
    r = run_bass_kernel_spmd(nc, [arrays], core_ids=[0])
    return r.results[0]["out_x"]
```

```python
import math
from contextlib import ExitStack

import concourse.bass as bass
from concourse import mybir

F32, I32, BF16 = mybir.dt.float32, mybir.dt.int32, mybir.dt.bfloat16
ALU = mybir.AluOpType
ACT = mybir.ActivationFunctionType
AX = mybir.AxisListType
ds = bass.ds

P = 128
N = 6250
E = 206250
D = 64
LAYERS = 4
AGGS = 6
DELTA = 2.5
EPS = 1e-5
TILES = -(-N // P)
TT = TILES + 1
HALF = TT // 2
DUMMY = TILES
LAST = N - (TILES - 1) * P
FC = HALF * P
VALID = ((HALF - 1) * P + LAST, (HALF - 1) * P)

BLOCK = 512
BLOCKS = -(-E // BLOCK)
SEARCHES = TILES + 1
LOAD_P = 75
LOAD_F = E // LOAD_P

ROUND = 64
WIN_STEP, WIN = 16, ROUND + 16
WINDOWS = E // WIN_STEP + 1
WIN_DIRECT = (E - WIN) // WIN_STEP + 1
TAIL0 = WIN_DIRECT * WIN_STEP
TAIL_REAL = E - TAIL0
TAIL = (WINDOWS - WIN_DIRECT - 1) * WIN_STEP + WIN

GROUP, SLOTS = 7, 4
BODY = GROUP * SLOTS
ITERS = -(-(ROUND + -(-E // P)) // BODY)
COLS = ITERS * BODY
FLATC = COLS + ROUND
BIG_TILES = -(-(E // (ROUND + 1)) // P)
BIG_GROUP = 4
BINS = ROUND + 2
BT = BINS * TILES
SCAN_CHUNKS = 7
SCAN = BT // SCAN_CHUNKS
PAY = D + 4
HUGE = 3.0e38
WIDE = 4 * P
FULL = VALID[1] // WIDE

A_AB, A_U, A_U0, A_MIX, A_BM, A_COL = 0, 128, 704, 768, 832, 896
A_ALL = A_COL + 6
NU = 3 * AGGS // 2
W_AB, W_U0, W_MIX, W_BM, W_COL, W_U = 0, 256, 384, 512, 576, 582
W_ALL = W_U + (2 * NU + 1) * D
C_BMIX, C_GT, C_BT, C_GO, C_BO, C_BU = (W_COL + i for i in range(6))
PAIRS = [(5, 0), (1, 2), (4, 3)]


def build(nc, x, src, dst, WM, bM, WU, bU, gamma_t, beta_t, Wmix, bmix, gamma_o, beta_o, out):
    assert BT == SCAN * SCAN_CHUNKS and SCAN <= 512 and VALID[1] == FULL * WIDE
    dst_f = nc.dram_tensor("dst_f", (BLOCKS, BLOCK), F32).ap()
    windows = nc.dram_tensor("windows", (WINDOWS, WIN), I32).ap()
    pos_d = nc.dram_tensor("pos_d", (TILES * P, PAY), F32).ap()
    table = nc.dram_tensor("table", (TILES * P, 2 * D), F32).ap()

    with ExitStack() as ctx:
        def sb(name, shape, dt=F32):
            return ctx.enter_context(nc.sbuf_tensor(name, shape, dt))

        def sem(name):
            return ctx.enter_context(nc.semaphore(name))

        onesf = sb("onesf", [P, SCAN])
        fold = sb("fold", [P, P])
        ones_bf = sb("ones_bf", [P, P], BF16)
        below_bf = sb("below_bf", [P, P], BF16)
        prefix = sb("prefix", [64, TT])
        tiny = sb("tiny", [P, 1])
        epsc = sb("epsc", [P, 1])
        weights = sb("weights", [P, LAYERS, A_ALL])
        W = sb("W", [P, W_ALL])

        flat = sb("flat", [P, 2, FLATC], I32)
        toff = sb("toff", [1, FLATC], I32)
        colo = sb("colo", [1, TT], I32)
        nid = sb("nid", [P, TILES], I32)
        rank_i = sb("rank_i", [P, TILES], I32)
        scal = sb("scal", [P, 8, TT])
        DEG, RDEN, HAS, AMP, ATT, TMP0, TMP1, LEN = (scal[:, k, :] for k in range(8))
        XP = sb("XP", [P, TILES, PAY])

        SS = sb("SS", [P, TT, 2 * D])
        MM = sb("MM", [P, TT, 2 * D])
        MS = sb("MS", [P, TT, 2 * D])
        B = sb("B", [P, TT, D])
        hT = sb("hT", [P, FC])
        HU = sb("HU", [P, TT, D])
        HUT = sb("HUT", [P, FC])
        rows = sb("rows", [P, BODY, 2 * D])
        idx = sb("idx", [P, BODY], I32)
        D3 = sb("D3", [P, 3 * P])
        SM = sb("SM", [P, 2 * D])
        QM = sb("QM", [P, 2 * D])
        XB = sb("XB", [P, 3 * D])
        MMH = sb("MMH", [P, 2 * D])
        VS = sb("VS", [P, 2 * D])
        negid = sb("negid", [P, P])
        ident = D3[:, 0:P]
        WS = sb("WS", [P, P])
        sums_u = sb("sums_u", [P, HALF])
        sums_o = sb("sums_o", [P, FULL + 1])
        col = sb("col", [P, 16])
        Z = MS[:, :, :].rearrange("p t f -> p (t f)")[:, 0:FC]
        OT = MS[:, :, :].rearrange("p t f -> p (t f)")[:, FC:2 * FC]
        AGT = MS[:, 0:9, :].rearrange("p (c s) n -> p c (s n)", c=3)
        JUNK = HU[:, :, :].rearrange("p t f -> p (t f)")
        bank = [ctx.enter_context(nc.psum_tensor(f"bank{i}", [P, 512], F32)) for i in range(8)]

        extra = sb("extra", [1, 1], I32)
        kb = sb("kb", [P, 1])
        binsf = sb("binsf", [P, ROUND + 2])
        LT = sb("LT", [64, 1])
        LT2 = sb("LT2", [P, 1])

        used = [0]

        def small(n, dt=F32, rows=P):
            used[0] += n
            assert used[0] <= FC
            v = HUT[0:rows, used[0] - n:used[0]]
            return v if dt == F32 else v.bitcast(dt)
        nd = small(SEARCHES)
        ndi = small(SEARCHES, I32)
        c1 = small(SEARCHES)
        c2 = small(SEARCHES)
        blki = small(SEARCHES, I32)
        rp = small(SEARCHES)
        key = small(TILES)
        binsi = small(ROUND + 2, I32)
        start_i = small(TILES, I32)
        win_i = small(TILES, I32)
        offb = small(4 * TILES, I32).rearrange("p (k t) -> p k t", k=4)
        pad_row = small(BLOCKS * BLOCK - E, rows=1)
        tail_i = small(TAIL, I32, rows=1)
        flatSS = SS[:, :, :].rearrange("p t f -> p (t f)")
        flatMM = MM[:, :, :].rearrange("p t f -> p (t f)")
        flatHU = HU[:, :, :].rearrange("p t f -> p (t f)")
        big = [flatHU[:, k * WIN:(k + 1) * WIN].bitcast(I32) for k in range(2)]
        big_past = flatHU[:, 2 * WIN:2 * WIN + ROUND].bitcast(I32)
        big_keep = flatHU[:, 2 * WIN + ROUND:2 * WIN + 2 * ROUND]
        b0 = 2 * WIN + 2 * ROUND
        big_start = flatHU[:, b0:b0 + 1]
        big_len = flatHU[:, b0 + 1:b0 + 2]
        big_i, big_win = (flatHU[:, b0 + k:b0 + k + 1].bitcast(I32) for k in (2, 3))
        big_off = flatHU[:, b0 + 4:b0 + 8].bitcast(I32)
        big_idx = flatHU[:, b0 + 8:b0 + 8 + BIG_GROUP].bitcast(I32)
        flatMS = MS[:, :, :].rearrange("p t f -> p (t f)")
        dst_i = flatSS[0:LOAD_P, 0:LOAD_F].bitcast(I32)
        dst_s = flatSS[0:LOAD_P, LOAD_F:2 * LOAD_F]
        samples_i = flatHU[0:1, 0:BLOCKS].bitcast(I32)
        samples = flatHU[0:1, BLOCKS:2 * BLOCKS]
        pay = flatMM[:, 0:TILES * PAY].rearrange("p (t f) -> p t f", f=PAY)
        found = flatMS[:, 0:7 * BLOCK].rearrange("p (s b) -> p s b", b=BLOCK)
        junk = flatMS[:, 7 * BLOCK:8 * BLOCK]
        shrug = B[:, :, :].rearrange("p t f -> p (t f)")[:, 0:10 * BLOCK // 2].bitcast(BF16).rearrange("p (s b) -> p s b", b=BLOCK)
        onehot = flatMS[:, 4096:4096 + BT // 2].bitcast(BF16)
        before = flatSS[:, 0:BT]
        winA = flatSS[:, 0:TILES * WIN].bitcast(I32).rearrange("p (t w) -> p t w", w=WIN)
        winB = flatMS[:, 0:TILES * WIN].bitcast(I32).rearrange("p (t w) -> p t w", w=WIN)
        pack = flatMM[:, 0:TILES * 2 * ROUND].bitcast(I32).rearrange("p (t k j) -> p t k j", k=2, j=ROUND)
        past = HU[:, 0:TILES, :].bitcast(I32)
        tvals = hT[0:1, 0:TT * ROUND].bitcast(I32).rearrange("p (t j) -> p t j", j=ROUND)
        bT = rows[:, :, :].rearrange("p c f -> p (c f)")[:, 0:BT]

        names = ("passed big_reset big_mx big_mx2 big_ready big_found big_rows kb_done big_v big_next big_added ld_x ld_w ld_dst ld_smp dstf_done dstf_st pad_st smp_done smp_ps c1_done win_st tail_ld "
                 "pool_c dve_c c2_done hot_done ps1 ps1_used ps2 rank_done pos_ld win_ld lenT lt_done colps colo_done "
                 "pack_done flat_done toff_done pay_done sc_pos xp_act h0_done h0_ps h0_ev v a "
                 "w_now a_ps b_ps b_done tab_ready tab_sc idx_ready added cls "
                 "tile_in v_ps var_done vs_done turned agt hu_ps hut_done mean_done sq_done var_sum fold_ps "
                 "aff1 ws_done zb_done leaky mix_ps z_done ot_done aff2 r_done h_next root fin_ps fin_ev fin_sc").split()
        S = {n: sem(n) for n in names}
        gat = [sem(f"gathered{i}") for i in range(SLOTS)]
        blk_s = [sem(f"block_found{i}") for i in range(7)]

        def wait(eng, s, value):
            eng.wait_ge(S[s] if isinstance(s, str) else s, value)
            if not isinstance(value, int):
                eng.sem_inc(S["passed"])

        def chained(eng, name):
            n = [0]

            def step(ins):
                n[0] += 1
                ins.then_inc(S[name], 1)
                eng.wait_ge(S[name], n[0])
            return step

        prep = nc.Block()
        block = prep.__enter__()

        @block.sync
        def _(sp):
            sp.dma_start(dst_i, dst.rearrange("(p f) -> p f", p=LOAD_P)).then_inc(S["ld_dst"], 16)
            with nc.allow_non_contiguous_dma(reason="one sample of each block"):
                sp.dma_start(samples_i[0:1, :], bass.AP(dst.tensor, 0, [[E, 1], [BLOCK, BLOCKS]])).then_inc(S["ld_smp"], 16)
            sp.wait_ge(S["dve_c"], 1)
            full = N // TILES
            sp.dma_start(pay[0:full, :, 0:D], x[0:full * TILES, :].rearrange("(p i) f -> p i f", i=TILES)).then_inc(S["ld_x"], 16)
            rest = N - full * TILES
            sp.dma_start(pay[full:full + 1, 0:rest, 0:D], x[full * TILES:N, :].rearrange("(p i) f -> p i f", p=1)).then_inc(S["ld_x"], 16)
            even = WIN_DIRECT // 16 * 16
            sp.dma_start(windows[0:even, :], bass.AP(src.tensor, 0, [[WIN_STEP, even], [1, WIN]])).then_inc(S["win_st"], 16)
            sp.dma_start(windows[even:WIN_DIRECT, :],
                         bass.AP(src.tensor, even * WIN_STEP, [[WIN_STEP, WIN_DIRECT - even], [1, WIN]])).then_inc(S["win_st"], 16)
            sp.dma_start(tail_i[0:1, 0:TAIL_REAL], src[TAIL0:E].rearrange("(p f) -> p f", p=1)).then_inc(S["tail_ld"], 16)
            sp.wait_ge(S["tail_ld"], 16)
            for i in range(WINDOWS - WIN_DIRECT):
                sp.dma_start(windows[WIN_DIRECT + i:WIN_DIRECT + i + 1, :],
                             tail_i[0:1, i * WIN_STEP:i * WIN_STEP + WIN]).then_inc(S["win_st"], 16)
            sp.wait_ge(S["dstf_done"], 1)
            sp.dma_start(bass.AP(dst_f.tensor, 0, [[LOAD_F, LOAD_P], [1, LOAD_F]]), dst_s).then_inc(S["dstf_st"], 16)
            sp.dma_start(bass.AP(dst_f.tensor, E, [[BLOCKS * BLOCK - E, 1], [1, BLOCKS * BLOCK - E]]), pad_row[0:1, :]).then_inc(S["dstf_st"], 16)
            sp.wait_ge(S["sc_pos"], 16 * TILES)
            sp.dma_start(XP[:, :, :], pos_d.rearrange("(t p) f -> p t f", p=P)).then_inc(S["pos_ld"], 16)

        @block.scalar
        def _(act):
            act.wait_ge(S["dve_c"], 1)
            for h in range(2):
                r = slice(64 * h, 64 * h + 64)
                w = weights[r, :, :]
                act.dma_start(w[:, :, A_AB:A_AB + 64], WM[:, 0:64, :].rearrange("l k n -> k l n")).then_inc(S["ld_w"], 16)
                act.dma_start(w[:, :, A_AB + 64:A_AB + 128], WM[:, 64:128, :].rearrange("l k n -> k l n")).then_inc(S["ld_w"], 16)
                act.dma_start(w[:, :, A_U0:A_U0 + 64], WU[:, 0:64, :].rearrange("l k n -> k l n")).then_inc(S["ld_w"], 16)
                act.dma_start(w[:, :, A_MIX:A_MIX + 64], Wmix.rearrange("l k n -> k l n")).then_inc(S["ld_w"], 16)
                for c, pair in enumerate(PAIRS):
                    for s in range(3):
                        k0 = 64 + s * AGGS * D + pair[h] * D
                        o = A_U + c * 192 + s * 64
                        act.dma_start(w[:, :, o:o + 64], WU[:, k0:k0 + D, :].rearrange("l k n -> k l n")).then_inc(S["ld_w"], 16)
                with nc.allow_non_contiguous_dma(reason="one value per partition"):
                    for o, v in ((C_BMIX, bmix), (C_GT, gamma_t), (C_BT, beta_t), (C_GO, gamma_o), (C_BO, beta_o), (C_BU, bU)):
                        act.dma_start(w[:, :, A_COL - W_COL + o:A_COL - W_COL + o + 1], v.rearrange("l (k n) -> k l n", n=1)).then_inc(S["ld_w"], 16)
            act.dma_start(weights[:, :, A_BM:A_BM + D], bass.AP(bM.tensor, 0, [[0, P], [D, LAYERS], [1, D]])).then_inc(S["ld_w"], 16)
            act.wait_ge(S["win_ld"], 1)
            nc.scalar.activation(TMP1, DEG, ACT.Ln, bias=onesf[:, 0:1]).then_inc(S["a"], 1)
            act.wait_ge(S["pack_done"], 1)
            act.wait_ge(S["colo_done"], 1)
            with act.Fori(0, TILES) as t:
                o = act.value_load(colo[0:1, ds(t, 1)], min_val=0, max_val=COLS)
                wait(act, "flat_done", t + 1)
                nc.scalar.copy(flat[:, :, ds(o, ROUND)],
                               pack[:, ds(t, 1), :, :].rearrange("p t k j -> p (t k) j")).then_inc(S["flat_done"], 1)
            act.wait_ge(S["h0_done"], 1)
            nc.scalar.activation(TMP0, TMP0, ACT.Sqrt).then_inc(S["a"], 1)

        @block.gpsimd
        def _(pool):
            nc.gpsimd.iota(ndi[:, :], pattern=[[1, SEARCHES]], base=0, channel_multiplier=TILES).then_inc(S["pool_c"], 1)
            nc.gpsimd.iota(binsi[:, :], pattern=[[1, BINS]], base=0, channel_multiplier=0).then_inc(S["pool_c"], 1)
            nc.gpsimd.iota(tvals[0:1, :, :], pattern=[[2 * D, TT], [0, ROUND]], base=0, channel_multiplier=0).then_inc(S["pool_c"], 1)
            pool.wait_ge(S["dve_c"], 1)
            nc.gpsimd.affine_select(out=ident, in_=onesf[:, 0:P], compare_op=ALU.is_equal, fill=0.0, base=0,
                                    pattern=[[-1, P]], channel_multiplier=1).then_inc(S["pool_c"], 1)
            nc.gpsimd.affine_select(out=junk[:, 0:P], in_=onesf[:, 0:P], compare_op=ALU.is_ge, fill=0.0, base=0,
                                    pattern=[[-1, P]], channel_multiplier=1).then_inc(S["pool_c"], 1)
            nc.gpsimd.affine_select(out=prefix[:, :], in_=onesf[0:64, 0:TT], compare_op=ALU.is_ge, fill=0.0, base=-1,
                                    pattern=[[1, TT]], channel_multiplier=-1).then_inc(S["pool_c"], 1)
            pool.wait_ge(S["dstf_st"], 32)
            for i in range(SEARCHES):
                if i % 10 == 0:
                    pool.wait_ge(S["c1_done"], i // 10 + 1)
                if i >= 7:
                    pool.wait_ge(S["c2_done"], i - 6)
                nc.gpsimd.indirect_dma_start(found[:, i % 7, :], None, dst_f,
                                             bass.IndirectOffsetOnAxis(ap=blki[:, i:i + 1], axis=0)).then_inc(blk_s[i % 7], 16)
            pool.wait_ge(S["rank_done"], 1)
            pool.wait_ge(S["ld_x"], 32)
            for i in range(TILES):
                nc.gpsimd.indirect_dma_start(pos_d, bass.IndirectOffsetOnAxis(ap=rank_i[:, i:i + 1], axis=0),
                                             pay[:, i, :], None).then_inc(S["sc_pos"], 16)
            pool.wait_ge(S["win_ld"], 1)
            pool.wait_ge(S["win_st"], 16 * (2 + WINDOWS - WIN_DIRECT))
            for t in range(TILES):
                nc.gpsimd.indirect_dma_start(winA[:, t, :], None, windows,
                                             bass.IndirectOffsetOnAxis(ap=win_i[:, t:t + 1], axis=0)).then_inc(blk_s[t // 7], 16)

        @block.vector
        def _(dve):
            step = chained(dve, "v")
            nc.vector.memset(onesf[:, :], 1.0)
            nc.vector.memset(ones_bf[:, :], 1.0)
            nc.vector.memset(tiny[:, :], 1e-30)
            nc.vector.memset(epsc[:, :], EPS)
            nc.vector.memset(pad_row[0:1, :], 1.0e9)
            nc.vector.memset(tail_i[0:1, :], 0)
            nc.vector.memset(W[:, :], 0.0)
            nc.vector.memset(sums_u[:, :], 0.0)
            nc.vector.memset(sums_o[:, :], 0.0)
            nc.vector.memset(col[:, :], 0.0)
            nc.vector.memset(scal[:, :, :], 0.0)
            nc.vector.memset(flat[:, :, :], 0)
            nc.vector.memset(toff[0:1, :], DUMMY * 2 * D)
            nc.vector.memset(pay[96:128, :, :], 0.0).then_inc(S["dve_c"], 1)
            dve.wait_ge(S["dve_c"], 1)
            nc.vector.nop().then_inc(S["flat_done"], 1)
            nc.vector.nop().then_inc(S["toff_done"], 1)
            nc.vector.nop().then_inc(S["big_added"], 1)
            nc.vector.nop().then_inc(S["added"], 1)
            nc.vector.nop().then_inc(S["hut_done"], 1)
            nc.vector.nop().then_inc(S["h_next"], FULL + 1)
            dve.wait_ge(S["ld_smp"], 16)
            nc.vector.tensor_copy(samples[0:1, :], samples_i[0:1, :]).then_inc(S["smp_done"], 1)
            dve.wait_ge(S["ld_dst"], 16)
            nc.vector.tensor_copy(dst_s, dst_i).then_inc(S["dstf_done"], 1)
            dve.wait_ge(S["pool_c"], 6)
            nc.vector.tensor_copy(binsf[:, :], binsi[:, :])
            nc.vector.tensor_scalar(below_bf[:, :], junk[:, 0:P], -1.0, None, ALU.mult)
            step(nc.vector.tensor_copy(nd[:, :], ndi[:, :]))
            nc.vector.tensor_scalar(negid[:, :], ident, -1.0, None, ALU.mult)
            nc.vector.tensor_copy(fold[:, 0:64], ident[:, 0:64])
            step(nc.vector.tensor_copy(fold[:, 64:128], ident[:, 64:128]))
            nc.vector.tensor_tensor(fold[:, 0:64], ident[:, 0:64], ident[:, 64:128], ALU.add)
            step(nc.vector.tensor_tensor(fold[:, 64:128], ident[:, 0:64], ident[:, 64:128], ALU.add))
            dve.wait_ge(S["smp_ps"], 1)
            for i in range(SEARCHES):
                ins = nc.vector.tensor_scalar(shrug[:, i % 10, 0:BLOCKS], bank[7][:, 0:BLOCKS], nd[:, i:i + 1], 0.0,
                                              ALU.is_lt, ALU.add, accum_out=c1[:, i:i + 1])
                if i % 10 == 9:
                    step(ins)
                    r = slice(i - 9, i + 1)
                    step(nc.vector.tensor_scalar(c1[:, r], c1[:, r], -1.0, 0.0, ALU.add, ALU.max))
                    nc.vector.tensor_copy(blki[:, r], c1[:, r]).then_inc(S["c1_done"], 1)
            for i in range(SEARCHES):
                dve.wait_ge(blk_s[i % 7], 16 * (i // 7 + 1))
                if i >= 10:
                    dve.wait_ge(S["c2_done"], i - 9)
                nc.vector.tensor_scalar(shrug[:, i % 10, :], found[:, i % 7, :], nd[:, i:i + 1], 0.0,
                                        ALU.is_lt, ALU.add, accum_out=c2[:, i:i + 1]).then_inc(S["c2_done"], 1)
            dve.wait_ge(S["c2_done"], SEARCHES)
            step(nc.vector.scalar_tensor_tensor(rp[:, :], c1[:, :], float(BLOCK), c2[:, :], ALU.mult, ALU.add))
            dve.wait_ge(S["ld_x"], 32)
            payc = pay.rearrange("p t f -> p f t")
            step(nc.vector.tensor_tensor(payc[:, D + 2, :], rp[:, 1:SEARCHES], rp[:, 0:TILES], ALU.subtract))
            nc.vector.tensor_copy(payc[:, D, :], nd[:, 0:TILES])
            nc.vector.tensor_copy(payc[:, D + 1, :], rp[:, 0:TILES])
            nc.vector.memset(payc[:, D + 3, :], 0.0)
            step(nc.vector.tensor_scalar(key[:, :], payc[:, D + 2, :], float(ROUND), -1.0, ALU.min, ALU.mult))
            step(nc.vector.tensor_scalar(c1[:, 0:TILES], nd[:, 0:TILES], float(N), float(ROUND), ALU.is_ge, ALU.add))
            step(nc.vector.tensor_tensor(key[:, :], key[:, :], c1[:, 0:TILES], ALU.add))
            hot = onehot.rearrange("p (c i) -> p c i", i=TILES)
            nc.vector.tensor_tensor(hot, key[:, :].unsqueeze(1).to_broadcast([P, BINS, TILES]),
                                    binsf[:, :].unsqueeze(2).to_broadcast([P, BINS, TILES]), ALU.is_equal).then_inc(S["hot_done"], 1)
            for k in range(SCAN_CHUNKS):
                dve.wait_ge(S["ps1"], k + 1)
                r = slice(k * SCAN, (k + 1) * SCAN)
                step(nc.vector.tensor_tensor_scan(before[:, r], onesf[:, 0:SCAN], bank[k][:, 0:SCAN],
                                                  before[:, k * SCAN - 1:k * SCAN] if k else 0.0, ALU.mult, ALU.add))
                nc.vector.nop().then_inc(S["ps1_used"], 1)
            for k in range(SCAN_CHUNKS):
                dve.wait_ge(S["ps2"], k + 1)
                r = slice(k * SCAN, (k + 1) * SCAN)
                step(nc.vector.tensor_tensor(bT[:, r], before[:, r], bank[k][:, 0:SCAN], ALU.add))
            step(nc.vector.tensor_tensor(bT, bT, onehot, ALU.mult))
            step(nc.vector.tensor_reduce(c2[:, 0:TILES], bT.rearrange("p (c i) -> p i c", i=TILES), AX.X, ALU.add))
            nc.vector.tensor_copy(rank_i[:, :], c2[:, 0:TILES]).then_inc(S["rank_done"], 1)

            dve.wait_ge(S["pos_ld"], 16)
            XC = XP[:, :, :].rearrange("p t f -> p f t")
            nc.vector.tensor_copy(nid[:, :], XC[:, D, :])
            nc.vector.tensor_copy(DEG[:, 0:TILES], XC[:, D + 2, :])
            step(nc.vector.tensor_copy(start_i[:, :], XC[:, D + 1, :]))
            nc.vector.tensor_scalar(LEN, DEG, float(ROUND), None, ALU.min)
            for k in range(4):
                nc.vector.tensor_scalar(offb[:, k, :], start_i[:, :], 8 >> k, None, ALU.bitwise_and)
            step(nc.vector.tensor_scalar(win_i[:, :], start_i[:, :], 4, None, ALU.arith_shift_right))
            nc.vector.nop().then_inc(S["win_ld"], 1)
            dve.wait_ge(S["lenT"], 1)
            step(nc.vector.tensor_reduce(LT[0:TILES, :], bank[0][0:TILES, 0:P], AX.X, ALU.max))
            nc.vector.nop().then_inc(S["lt_done"], 1)
            step(nc.vector.tensor_tensor(past, binsf[:, 0:ROUND].unsqueeze(1).to_broadcast([P, TILES, ROUND]),
                                         LEN[:, 0:TILES].unsqueeze(2).to_broadcast([P, TILES, ROUND]), ALU.is_ge))
            step(nc.vector.tensor_scalar(pack[:, :, 1, :], past, -1.0, 1.0, ALU.mult, ALU.add))
            step(nc.vector.tensor_reduce(LT2[:, :], DEG, AX.X, ALU.max))
            nc.vector.nop().then_inc(S["big_mx"], 1)
            dve.wait_ge(S["big_mx2"], 1)
            step(nc.vector.tensor_reduce(LT2[0:1, :], bank[2][0:1, 0:P], AX.X, ALU.max))
            step(nc.vector.tensor_scalar(extra[0:1, :], LT2[0:1, :], -1.0, 0.0, ALU.add, ALU.max))
            step(nc.vector.tensor_scalar(extra[0:1, :], extra[0:1, :], ROUND.bit_length() - 1, None, ALU.arith_shift_right))
            dve.wait_ge(S["colps"], 1)
            step(nc.vector.tensor_copy(colo[0:1, :], bank[1][0:1, 0:TT]))
            nc.vector.nop().then_inc(S["colo_done"], 1)
            for t in range(TILES):
                if t % 7 == 0:
                    g = t // 7
                    dve.wait_ge(blk_s[g], 16 * (len(range(g, SEARCHES, 7)) + 7))
            cur, nxt, w = winA, winB, WIN
            for k in range(4):
                s = 8 >> k
                w -= s
                step(nc.vector.tensor_copy(nxt[:, :, 0:w], cur[:, :, 0:w]))
                step(nc.vector.copy_predicated(nxt[:, :, 0:w], offb[:, k, :].unsqueeze(2).to_broadcast([P, TILES, w]),
                                               cur[:, :, s:s + w]))
                cur, nxt = nxt, cur
            step(nc.vector.tensor_copy(pack[:, :, 0, :], cur[:, :, 0:ROUND]))
            step(nc.vector.copy_predicated(pack[:, :, 0, :], past, cur[:, :, 0:1].to_broadcast([P, TILES, ROUND])))
            nc.vector.nop().then_inc(S["pack_done"], 1)
            with dve.Fori(0, TT) as t:
                o = dve.value_load(colo[0:1, ds(t, 1)], min_val=0, max_val=COLS)
                wait(dve, "toff_done", t + 1)
                nc.vector.tensor_copy(toff[0:1, ds(o, ROUND)],
                                      tvals[0:1, ds(t, 1), :].rearrange("p t j -> p (t j)")).then_inc(S["toff_done"], 1)
            dve.wait_ge(S["flat_done"], TILES + 1)
            nc.vector.tensor_copy(flat[:, 0, COLS:COLS + BODY], flat[:, 0, 0:BODY])
            nc.vector.tensor_copy(idx[:, :], flat[:, 0, 0:BODY]).then_inc(S["idx_ready"], SLOTS)
            nc.vector.tensor_scalar(HAS, DEG, 1.0, None, ALU.min)
            step(nc.vector.tensor_scalar(TMP0, DEG, 1.0, None, ALU.max))
            step(nc.vector.reciprocal(RDEN, TMP0))
            dve.wait_ge(S["a"], 1)
            nc.vector.tensor_scalar(AMP, TMP1, 1.0 / DELTA, None, ALU.mult)
            step(nc.vector.tensor_scalar(TMP0, TMP1, 0.5, None, ALU.max))
            step(nc.vector.reciprocal(TMP0, TMP0))
            step(nc.vector.scalar_tensor_tensor(ATT, TMP0, DELTA, HAS, ALU.mult, ALU.mult))
            x3 = XP[:, :, 0:D]
            h0 = B[:, 0:TILES, :]
            b3 = [P, TILES, D]
            nc.vector.memset(B[:, TILES, :], 0.0)
            step(nc.vector.tensor_reduce(TMP0[:, 0:TILES], x3, AX.X, ALU.add))
            step(nc.vector.tensor_scalar(TMP0, TMP0, 1.0 / D, None, ALU.mult))
            step(nc.vector.tensor_tensor(h0, x3, TMP0[:, 0:TILES].unsqueeze(2).to_broadcast(b3), ALU.subtract))
            step(nc.vector.tensor_tensor(HU[:, 0:TILES, :], h0, h0, ALU.mult))
            step(nc.vector.tensor_reduce(TMP0[:, 0:TILES], HU[:, 0:TILES, :], AX.X, ALU.add))
            step(nc.vector.tensor_scalar(TMP0, TMP0, 1.0 / D, EPS, ALU.mult, ALU.add))
            nc.vector.nop().then_inc(S["h0_done"], 1)
            dve.wait_ge(S["a"], 2)
            step(nc.vector.reciprocal(TMP1, TMP0))
            step(nc.vector.tensor_tensor(h0, h0, TMP1[:, 0:TILES].unsqueeze(2).to_broadcast(b3), ALU.mult))
            step(nc.vector.tensor_scalar(B[:, :, :], B[:, :, :], 0.0, None, ALU.max))
            nc.vector.nop().then_inc(S["h0_done"], 1)
            for j in range(HALF):
                dve.wait_ge(S["h0_ps"], j + 1)
                nc.vector.tensor_copy(hT[:, j * P:(j + 1) * P], bank[2 + j % 2][:, 0:P]).then_inc(S["h0_ev"], 1)

        @block.tensor
        def _(pe):
            pe.wait_ge(S["smp_done"], 1)
            pe.wait_ge(S["dve_c"], 1)
            nc.tensor.matmul(bank[7][:, 0:BLOCKS], onesf[0:1, 0:P], samples[0:1, :], start=True, stop=True).then_inc(S["smp_ps"], 1)
            pe.wait_ge(S["hot_done"], 1)
            for k in range(SCAN_CHUNKS):
                nc.tensor.matmul(bank[k][:, 0:SCAN], ones_bf[:, :], onehot[:, k * SCAN:(k + 1) * SCAN],
                                 start=True, stop=True).then_inc(S["ps1"], 1)
            for k in range(SCAN_CHUNKS):
                pe.wait_ge(S["ps1_used"], k + 1)
                nc.tensor.matmul(bank[k][:, 0:SCAN], below_bf[:, :], onehot[:, k * SCAN:(k + 1) * SCAN],
                                 start=True, stop=True).then_inc(S["ps2"], 1)
            pe.wait_ge(S["win_ld"], 1)
            nc.tensor.transpose(bank[0][0:TILES, 0:P], LEN[:, 0:TILES], ident).then_inc(S["lenT"], 1)
            pe.wait_ge(S["lt_done"], 1)
            nc.tensor.matmul(bank[1][0:1, 0:TT], LT[0:TILES, :], prefix[0:TILES, :], start=True, stop=True).then_inc(S["colps"], 1)
            pe.wait_ge(S["big_mx"], 1)
            nc.tensor.transpose(bank[2][0:1, 0:P], LT2[:, :], ident).then_inc(S["big_mx2"], 1)
            pe.wait_ge(S["h0_done"], 2)
            for j in range(HALF):
                if j >= 2:
                    pe.wait_ge(S["h0_ev"], j - 1)
                nc.tensor.transpose(bank[2 + j % 2][:, 0:P], B[:, 2 * j:2 * j + 2, :], ident).then_inc(S["h0_ps"], 1)
        prep.__exit__(None, None, None)

        block = ctx.enter_context(nc.Block())

        sums = SS[:, :, :].rearrange("p t f -> p (t f)")
        exts = MM[:, :, :].rearrange("p t f -> p (t f)")

        BIG_STEPS = 17
        STEPS_ALL = 8
        h3 = hT[:, :].rearrange("p (j n) -> p j n", n=P)
        HUT3 = HUT[:, :].rearrange("p (j n) -> p j n", n=P)
        XPx = XP[:, :, 0:D]
        c_nmu, c_std, c_rstd, c_scale, c_bias, c_zb, c_sum, c_var = (col[:, k:k + 1] for k in range(8))
        c_sq = col[:, 8:10]
        rest = slice(VALID[1], VALID[0])
        steps = [slice(m * WIDE, min((m + 1) * WIDE, FC)) for m in range(FULL + 1)]

        def load_offsets(dve, c0):
            _, values = nc.values_load_multi_w_load_instructions(
                toff[0:1, ds(c0, GROUP)], engines=[mybir.EngineType.DVE], min_val=0, max_val=DUMMY * 2 * D,
                skip_runtime_bounds_check_because="toff holds tile numbers up to DUMMY, times 2 * D")
            return values

        @block.sync
        def _(sp):
            sp.wait_ge(S["fin_sc"], 16 * TILES)

        @block.gpsimd
        def _(pool):
            more = pool.value_load(extra[0:1, 0:1], min_val=0, max_val=E // ROUND)
            with pool.Fori(0, LAYERS) as l:
                for t in range(TILES):
                    if t % 8 == 0:
                        wait(pool, "tab_ready", l * (FULL + 1) + t // 8 + 1)
                    nc.gpsimd.indirect_dma_start(table, bass.IndirectOffsetOnAxis(ap=nid[:, t:t + 1], axis=0),
                                                 MS[:, t, :], None).then_inc(S["tab_sc"], 16)
                wait(pool, "tab_sc", l * (16 * TILES) + 16 * TILES)
                with pool.If(more > 0):
                    with pool.Fori(0, more) as k:
                        with pool.Fori(0, BIG_TILES) as t:
                            n = (l * more + k) * BIG_TILES + t
                            wait(pool, "big_ready", n + 1)
                            nc.gpsimd.indirect_dma_start(big[0], None, windows,
                                                         bass.IndirectOffsetOnAxis(ap=big_win, axis=0)).then_inc(S["big_found"], 16)
                            with pool.Fori(0, ROUND // BIG_GROUP) as q:
                                wait(pool, "big_next", n * (ROUND // BIG_GROUP) + q + 1)
                                for c in range(BIG_GROUP):
                                    nc.gpsimd.indirect_dma_start(rows[:, c, :], None, table,
                                                                 bass.IndirectOffsetOnAxis(ap=big_idx[:, c:c + 1], axis=0)).then_inc(S["big_rows"], 16)
                            wait(pool, "big_added", (n + 1) * ROUND + 1)
                            nc.gpsimd.inc_swdge_sem([S["big_found"], S["big_rows"]], [16, 16 * ROUND], mode="sub")
                            pool.sem_inc(S["big_reset"])
                    pool.sem_inc(S["passed"])
                with pool.Fori(0, ITERS) as i:
                    for b in range(SLOTS):
                        wait(pool, "idx_ready", l * (ITERS * SLOTS) + i * SLOTS + b + 1)
                        for k in range(b * GROUP, (b + 1) * GROUP):
                            nc.gpsimd.indirect_dma_start(rows[:, k, :], None, table,
                                                         bass.IndirectOffsetOnAxis(ap=idx[:, k:k + 1], axis=0)).then_inc(gat[b], 16)
            for t in range(TILES):
                if t % 2 == 0:
                    pool.wait_ge(S["fin_ev"], t // 2 + 1)
                nc.gpsimd.indirect_dma_start(out, bass.IndirectOffsetOnAxis(ap=nid[:, t:t + 1], axis=0),
                                             HU[:, t, :], None, bounds_check=N - 1, oob_is_err=False).then_inc(S["fin_sc"], 16)

        @block.scalar
        def _(act):
            with act.Fori(0, LAYERS) as l:
                for m in range(FULL + 1):
                    t0, n = 8 * m, min(8, TT - 8 * m)
                    wait(act, "a_ps", l * (FULL + 1) + m + 1)
                    a3 = bank[5 + m % 2][:, 0:n * D].rearrange("p (t f) -> p t f", f=D)
                    nc.scalar.copy(MS[:, t0:t0 + n, 0:D], a3)
                    nc.scalar.activation(MS[:, t0:t0 + n, D:2 * D], a3, ACT.Square).then_inc(S["tab_ready"], 1)

                def tile(t):
                    k = l * TILES + t
                    at = ds(t, 1)
                    flat2 = lambda v: v[:, at, :].rearrange("p t f -> p (t f)")
                    end = act.value_load(colo[0:1, ds(t + 1, 1)], min_val=0, max_val=COLS)
                    wait(act, "added", l * COLS + end + 1)
                    s, q, b = sums[:, ds(t * (2 * D), D)], sums[:, ds(t * (2 * D) + D, D)], flat2(B)
                    nc.scalar.mul(QM[:, 0:D], q, RDEN[:, at])
                    nc.scalar.activation(QM[:, D:2 * D], s, ACT.Square, scale=RDEN[:, at])
                    nc.scalar.mul(XB[:, 0:D], b, DEG[:, at])
                    nc.scalar.mul(XB[:, D:2 * D], b, HAS[:, at])
                    nc.scalar.mul(XB[:, 2 * D:3 * D], b, HAS[:, at])
                    nc.scalar.mul(MMH[:, :], flat2(MM), HAS[:, at])
                    nc.scalar.mul(D3[:, P:2 * P], ident, AMP[:, at])
                    nc.scalar.mul(D3[:, 2 * P:3 * P], ident, ATT[:, at])
                    nc.scalar.copy(SM[:, 0:D], s)
                    nc.scalar.mul(SM[:, D:2 * D], s, RDEN[:, at]).then_inc(S["tile_in"], 1)
                    wait(act, "v_ps", k + 1)
                    nc.scalar.activation(VS[:, 0:D], bank[0][:, 0:D], ACT.Relu).then_inc(S["var_done"], 1)
                    wait(act, "var_done", k + 1)
                    nc.scalar.activation(VS[:, D:2 * D], VS[:, 0:D], ACT.Sqrt, bias=tiny[:, :]).then_inc(S["vs_done"], 1)
                    for c in range(3):
                        wait(act, "turned", 3 * k + c + 1)
                        nc.scalar.copy(AGT[:, c, :], bank[1 + c][:, 0:3 * P]).then_inc(S["agt"], 1)

                with act.Fori(0, HALF - 1) as j:
                    tile(2 * j)
                    tile(2 * j + 1)
                    wait(act, "hu_ps", l * HALF + j + 1)
                    nc.scalar.activation(HUT[:, ds(j * P, P)], bank[4][:, 0:P], ACT.Identity, bias=W[:, C_BU:C_BU + 1],
                                         accum_out=sums_u[:, ds(j, 1)]).then_inc(S["hut_done"], 1)
                tile(TILES - 1)
                wait(act, "hu_ps", (l + 1) * HALF)
                nc.scalar.activation(HUT[:, VALID[1]:FC], bank[4][:, 0:P], ACT.Identity, bias=W[:, C_BU:C_BU + 1])
                nc.scalar.activation(OT[0:64, 0:LAST], bank[4][0:64, 0:LAST], ACT.Identity, bias=W[0:64, C_BU:C_BU + 1],
                                     accum_out=sums_u[0:64, HALF - 1:HALF]).then_inc(S["hut_done"], 1)

                def norm(n, src, scale2):
                    wait(act, "mean_done", l * 2 + n + 1)
                    nc.scalar.activation(JUNK[:, 0:VALID[1]], src[:, 0:VALID[1]], ACT.Square, bias=c_nmu,
                                         accum_out=c_sq[:, 0:1])
                    nc.scalar.activation(JUNK[0:64, rest], src[0:64, rest], ACT.Square, bias=c_nmu[0:64, :],
                                         accum_out=c_sq[0:64, 1:2]).then_inc(S["sq_done"], 1)
                    wait(act, "var_sum", l * 2 + n + 1)
                    nc.scalar.activation(c_std, c_var, ACT.Sqrt, bias=epsc[:, :], scale=scale2 / N).then_inc(S["root"], 1)

                norm(0, HUT, 1.0 / N)
                wait(act, "zb_done", l + 1)
                for m, r in enumerate(steps):
                    wait(act, "mix_ps", l * len(steps) + m + 1)
                    nc.scalar.activation(Z[:, r], bank[m % 4][:, 0:r.stop - r.start], ACT.Identity, bias=c_zb).then_inc(S["z_done"], 1)
                norm(1, OT, 1.0)
                wait(act, "aff2", l + 1)
                for r in steps:
                    nc.scalar.activation(OT[:, r], OT[:, r], ACT.Relu, bias=c_bias, scale=c_scale).then_inc(S["r_done"], 1)

        @block.vector
        def _(dve):
            dve.wait_ge(S["ld_w"], 16 * (2 * (4 + NU + 6) + 1))

            def further_rounds(l):
                nc.vector.memset(kb[:, :], float(ROUND)).then_inc(S["kb_done"], 1)
                wait(dve, "kb_done", (l * (more + 1)) + 1)
                with dve.Fori(0, more) as k:
                    with dve.Fori(0, BIG_TILES) as t:
                        n = (l * more + k) * BIG_TILES + t
                        count = [0]

                        def step(ins):
                            count[0] += 1
                            ins.then_inc(S["big_v"], 1)
                            wait(dve, "big_v", n * BIG_STEPS + count[0])

                        deg = DEG[:, ds(t, 1)]
                        first = XP[:, ds(t, 1), D + 1:D + 2].rearrange("p t f -> p (t f)")
                        step(nc.vector.tensor_scalar(big_start, deg, -1.0, 0.0, ALU.add, ALU.max))
                        step(nc.vector.tensor_scalar(big_start, big_start, kb[:, :], None, ALU.min))
                        step(nc.vector.tensor_tensor(big_start, big_start, first, ALU.add))
                        step(nc.vector.tensor_scalar(big_len, deg, kb[:, :], None, ALU.subtract))
                        step(nc.vector.tensor_copy(big_i, big_start))
                        for b in range(4):
                            nc.vector.tensor_scalar(big_off[:, b:b + 1], big_i, 8 >> b, None, ALU.bitwise_and)
                        nc.vector.tensor_scalar(big_past, binsf[:, 0:ROUND], big_len, None, ALU.is_ge)
                        step(nc.vector.tensor_scalar(big_win, big_i, 4, None, ALU.arith_shift_right))
                        step(nc.vector.tensor_scalar(big_keep, big_past, -1.0, 1.0, ALU.mult, ALU.add))
                        nc.vector.nop().then_inc(S["big_ready"], 1)
                        dve.wait_ge(S["big_found"], 16)
                        cur, nxt, w = *big, WIN
                        for b in range(4):
                            s = 8 >> b
                            w -= s
                            step(nc.vector.tensor_copy(nxt[:, 0:w], cur[:, 0:w]))
                            step(nc.vector.copy_predicated(nxt[:, 0:w], big_off[:, b:b + 1].to_broadcast([P, w]), cur[:, s:s + w]))
                            cur, nxt = nxt, cur
                        step(nc.vector.tensor_copy(nxt[:, 0:ROUND], cur[:, 0:ROUND]))
                        step(nc.vector.copy_predicated(nxt[:, 0:ROUND], big_past, cur[:, 0:1].to_broadcast([P, ROUND])))
                        assert count[0] == BIG_STEPS, count[0]
                        with dve.Fori(0, ROUND // BIG_GROUP) as q:
                            m = n * (ROUND // BIG_GROUP) + q
                            nc.vector.tensor_copy(big_idx, nxt[:, ds(q * BIG_GROUP, BIG_GROUP)]).then_inc(S["big_next"], 1)
                            wait(dve, "big_rows", q * (16 * BIG_GROUP) + 16 * BIG_GROUP)
                            for c in range(BIG_GROUP):
                                row = rows[:, c, :]
                                wait(dve, "big_added", m * BIG_GROUP + c + 1)
                                nc.vector.scalar_tensor_tensor(sums[:, ds(t * (2 * D), 2 * D)], row, big_keep[:, ds(q * BIG_GROUP + c, 1)],
                                                               sums[:, ds(t * (2 * D), 2 * D)], ALU.mult, ALU.add)
                                nc.vector.tensor_tensor(exts[:, ds(t * (2 * D), D)], exts[:, ds(t * (2 * D), D)], row[:, 0:D], ALU.max)
                                nc.vector.tensor_tensor(exts[:, ds(t * (2 * D) + D, D)], exts[:, ds(t * (2 * D) + D, D)], row[:, 0:D],
                                                        ALU.min).then_inc(S["big_added"], 1)
                        wait(dve, "big_reset", n + 1)
                    nc.vector.tensor_scalar(kb[:, :], kb[:, :], float(ROUND), None, ALU.add).then_inc(S["kb_done"], 1)
                    wait(dve, "kb_done", l * (more + 1) + k + 2)
                wait(dve, "big_added", (l * more + more) * (BIG_TILES * ROUND) + 1)

            more = dve.value_load(extra[0:1, 0:1], min_val=0, max_val=E // ROUND)
            with dve.Fori(0, LAYERS) as l:
                n_step = [0]

                def step(ins):
                    n_step[0] += 1
                    ins.then_inc(S["cls"], 1)
                    wait(dve, "cls", l * STEPS_ALL + n_step[0])

                now = weights[:, ds(l, 1), :].rearrange("p l w -> p (l w)")
                for h in range(2):
                    r = slice(64 * h, 64 * h + 64)
                    for o, a in ((W_AB + 64 * h, A_AB), (W_AB + 128 + 64 * h, A_AB + 64), (W_U0 + 64 * h, A_U0), (W_MIX + 64 * h, A_MIX)):
                        nc.vector.tensor_copy(W[r, o:o + 64], now[r, a:a + 64])
                nc.vector.tensor_copy(W[:, W_U:W_U + 2 * NU * D].rearrange("p (i z f) -> p i z f", z=2, f=D)[:, :, 1, :],
                                      now[:, A_U:A_U + NU * D].rearrange("p (i f) -> p i f", f=D))
                nc.vector.tensor_copy(W[:, W_BM:W_U], now[:, A_BM:A_ALL]).then_inc(S["w_now"], 1)
                wait(dve, "w_now", l + 1)
                for m in range(FULL + 1):
                    t0, n = 8 * m, min(8, TT - 8 * m)
                    wait(dve, "b_ps", l * (FULL + 1) + m + 1)
                    nc.vector.tensor_tensor(B[:, t0:t0 + n, :], bank[1 + m % 2][:, 0:n * D].rearrange("p (t f) -> p t f", f=D),
                                            W[:, W_BM:W_BM + D].unsqueeze(1).to_broadcast([P, n, D]), ALU.add).then_inc(S["b_done"], 1)
                nc.vector.memset(SS[:, :, :], 0.0)
                nc.vector.memset(MM[:, :, 0:D], -HUGE)
                step(nc.vector.memset(MM[:, :, D:2 * D], HUGE))
                with dve.If(more > 0):
                    further_rounds(l)
                with dve.Fori(0, ITERS) as i:
                    for b in range(SLOTS):
                        c0 = i * BODY + b * GROUP
                        wait(dve, gat[b], (l * ITERS + i) * (16 * GROUP) + 16 * GROUP)
                        offs = load_offsets(dve, c0)
                        for k in range(GROUP):
                            row, o = rows[:, b * GROUP + k, :], offs[k]
                            dve.wait_ge(S["added"], l * COLS + c0 + k + 1)
                            nc.vector.scalar_tensor_tensor(sums[:, ds(o, 2 * D)], row, flat[:, 1, ds(c0 + k, 1)],
                                                           sums[:, ds(o, 2 * D)], ALU.mult, ALU.add)
                            nc.vector.tensor_tensor(exts[:, ds(o, D)], exts[:, ds(o, D)], row[:, 0:D], ALU.max)
                            ins = nc.vector.tensor_tensor(exts[:, ds(o + D, D)], exts[:, ds(o + D, D)], row[:, 0:D], ALU.min)
                            ins.then_inc(S["added"], 1)
                        nc.vector.tensor_copy(idx[:, b * GROUP:(b + 1) * GROUP],
                                              flat[:, 0, ds(c0 + BODY, GROUP)]).then_inc(S["idx_ready"], 1)

                def norm(n, parts, scale2, gam, bet):
                    wait(dve, "fold_ps", l * 5 + 2 * n + 1 + (n > 0))
                    step(nc.vector.tensor_reduce(c_sum, bank[7][:, 0:parts], AX.X, ALU.add))
                    nc.vector.tensor_scalar(c_nmu, c_sum, -1.0 / N, None, ALU.mult).then_inc(S["mean_done"], 1)
                    wait(dve, "fold_ps", l * 5 + 2 * n + 2 + (n > 0))
                    nc.vector.tensor_reduce(c_var, bank[7][:, 0:2], AX.X, ALU.add).then_inc(S["var_sum"], 1)
                    wait(dve, "root", l * 2 + n + 1)
                    step(nc.vector.reciprocal(c_rstd, c_std))
                    step(nc.vector.tensor_scalar(c_scale, c_rstd, W[:, gam:gam + 1], math.sqrt(scale2), ALU.mult, ALU.mult))
                    return nc.vector.scalar_tensor_tensor(c_bias, c_nmu, c_scale, W[:, bet:bet + 1], ALU.mult, ALU.add)

                norm(0, HALF, 1.0 / N, C_GT, C_BT).then_inc(S["aff1"], 1)
                nc.vector.tensor_scalar(WS[:, :], W[:, W_MIX:W_MIX + P], c_scale, None, ALU.mult).then_inc(S["ws_done"], 1)
                wait(dve, "fold_ps", l * 5 + 3)
                nc.vector.tensor_tensor(c_zb, bank[7][:, 0:1], W[:, C_BMIX:C_BMIX + 1], ALU.add).then_inc(S["zb_done"], 1)
                for m in range(len(steps) + 1):
                    if m < len(steps):
                        r = steps[m]
                        wait(dve, "z_done", l * len(steps) + m + 1)
                        nc.vector.scalar_tensor_tensor(Z[:, r], Z[:, r], 0.01, Z[:, r], ALU.mult, ALU.max).then_inc(S["leaky"], 1)
                    if m == 0:
                        continue
                    r = steps[m - 1]
                    wait(dve, "leaky", l * len(steps) + m)
                    if m - 1 < FULL:
                        nc.vector.scalar_tensor_tensor(OT[:, r], Z[:, r], 1.0, hT[:, r], ALU.mult, ALU.add,
                                                       accum_out=sums_o[:, m - 1:m])
                    else:
                        step(nc.vector.tensor_tensor(OT[:, r], Z[:, r], hT[:, r], ALU.add))
                        ins = nc.vector.tensor_reduce(sums_o[0:64, m - 1:m], OT[0:64, rest], AX.X, ALU.add)
                ins.then_inc(S["ot_done"], 1)
                norm(1, FULL + 1, 1.0, C_GO, C_BO).then_inc(S["aff2"], 1)
                for m, r in enumerate(steps):
                    wait(dve, "r_done", l * len(steps) + m + 1)
                    nc.vector.tensor_tensor(hT[:, r], OT[:, r], hT[:, r], ALU.add).then_inc(S["h_next"], 1)
                assert n_step[0] == STEPS_ALL, n_step[0]
            for j in range(HALF):
                dve.wait_ge(S["fin_ps"], j + 1)
                n = min(2, TILES - 2 * j)
                nc.vector.tensor_tensor(HU[:, 2 * j:2 * j + n, :], bank[j % 2][:, 0:n * D].rearrange("p (a f) -> p a f", a=n),
                                        XPx[:, 2 * j:2 * j + n, :], ALU.add).then_inc(S["fin_ev"], 1)

        @block.tensor
        def _(pe):
            with pe.Fori(0, LAYERS) as l:
                wait(pe, "w_now", l + 1)

                def project(out_bank, w, ready, done):
                    for m, r in enumerate(steps):
                        if ready == "tab_ready":
                            wait(pe, "h_next", l * len(steps) + m + 1)
                        if m >= 2:
                            wait(pe, ready, l * (FULL + 1) + m - 1)
                        for j in range(r.start // P, r.stop // P):
                            o = (j % 4) * P
                            ins = nc.tensor.matmul(bank[out_bank + m % 2][:, o:o + P], h3[:, j, :], W[:, w:w + P], start=True, stop=True)
                        ins.then_inc(S[done], 1)
                project(5, W_AB, "tab_ready", "a_ps")
                project(1, W_AB + P, "b_done", "b_ps")
                wait(pe, "b_done", (l + 1) * (FULL + 1))

                def tile(t, half, last):
                    k = l * TILES + t
                    wait(pe, "tile_in", k + 1)
                    nc.tensor.matmul(bank[0][:, 0:D], ident, QM[:, 0:D], start=True, stop=False)
                    nc.tensor.matmul(bank[0][:, 0:D], negid[:, :], QM[:, D:2 * D], start=False, stop=True).then_inc(S["v_ps"], 1)
                    nc.tensor.matmul(bank[1][:, 0:3 * P], SM[:, :], D3[:, :], start=True, stop=False)
                    nc.tensor.matmul(bank[1][:, 0:3 * P], XB[:, 0:2 * D], D3[:, :], start=False, stop=True).then_inc(S["turned"], 1)
                    nc.tensor.matmul(bank[2][:, 0:3 * P], MMH[:, :], D3[:, :], start=True, stop=False)
                    nc.tensor.matmul(bank[2][:, 0:3 * P], XB[:, D:3 * D], D3[:, :], start=False, stop=True).then_inc(S["turned"], 1)
                    wait(pe, "vs_done", k + 1)
                    nc.tensor.matmul(bank[3][:, 0:3 * P], VS[:, :], D3[:, :], start=True, stop=True).then_inc(S["turned"], 1)
                    for c in range(3):
                        wait(pe, "agt", 3 * k + c + 1)
                        for i in range(3):
                            w = W_U + (2 * (3 * c + i) + (1 - half)) * D
                            ins = nc.tensor.matmul(bank[4][:, 0:P], W[:, w:w + P], AGT[:, c, i * P:(i + 1) * P],
                                                   start=False, stop=last and c == 2 and i == 2)
                    if last:
                        ins.then_inc(S["hu_ps"], 1)

                def own(j):
                    nc.tensor.matmul(bank[4][:, 0:P], W[:, W_U0:W_U0 + P], hT[:, ds(j * P, P)], start=True, stop=False)

                with pe.Fori(0, HALF - 1) as j:
                    wait(pe, "hut_done", l * HALF + j + 1)
                    own(j)
                    tile(2 * j, 0, False)
                    tile(2 * j + 1, 1, True)
                wait(pe, "hut_done", (l + 1) * HALF)
                own(HALF - 1)
                tile(TILES - 1, 0, True)

                wait(pe, "hut_done", (l + 1) * HALF + 1)
                nc.tensor.matmul(bank[7][:, 0:HALF], fold[:, :], sums_u[:, :], start=True, stop=True).then_inc(S["fold_ps"], 1)
                wait(pe, "sq_done", l * 2 + 1)
                nc.tensor.matmul(bank[7][:, 0:2], fold[:, :], c_sq, start=True, stop=True).then_inc(S["fold_ps"], 1)
                wait(pe, "aff1", l + 1)
                nc.tensor.matmul(bank[7][:, 0:1], W[:, W_MIX:W_MIX + P], c_bias, start=True, stop=True).then_inc(S["fold_ps"], 1)
                wait(pe, "ws_done", l + 1)
                for m, r in enumerate(steps):
                    if m >= 4:
                        wait(pe, "z_done", l * len(steps) + m - 3)
                    nc.tensor.matmul(bank[m % 4][:, 0:r.stop - r.start], WS[:, :], HUT[:, r], start=True, stop=True).then_inc(S["mix_ps"], 1)
                wait(pe, "ot_done", l + 1)
                nc.tensor.matmul(bank[7][:, 0:FULL + 1], fold[:, :], sums_o[:, :], start=True, stop=True).then_inc(S["fold_ps"], 1)
                wait(pe, "sq_done", l * 2 + 2)
                nc.tensor.matmul(bank[7][:, 0:2], fold[:, :], c_sq, start=True, stop=True).then_inc(S["fold_ps"], 1)
            pe.wait_ge(S["h_next"], (LAYERS + 1) * (FULL + 1))
            for j in range(HALF):
                if j >= 2:
                    pe.wait_ge(S["fin_ev"], j - 1)
                nc.tensor.transpose(bank[j % 2][:, 0:P], h3[:, j, :], ident).then_inc(S["fin_ps"], 1)


_INS = ["x", "src", "dst", "WM", "bM", "WU", "bU", "gamma_t", "beta_t", "Wmix", "bmix", "gamma_o", "beta_o"]


def kernel(**inputs):
    import numpy as np
    import concourse.bacc as bacc
    from concourse.bass_utils import run_bass_kernel_spmd

    nc = bacc.Bacc("TRN2", target_bir_lowering=False, num_devices=1)
    arrays, args = {}, []
    for name in _INS:
        a = np.ascontiguousarray(inputs[name if name in ("x", "src", "dst") else "L0_gnn_" + name])
        arrays[f"in_{name}"] = a
        args.append(nc.dram_tensor(f"in_{name}", a.shape, mybir.dt.from_np(a.dtype), kind="ExternalInput").ap())
    out = nc.dram_tensor("out_x", (N, D), F32, kind="ExternalOutput").ap()
    build(nc, *args, out)
    r = run_bass_kernel_spmd(nc, [arrays], core_ids=[0])
    return r.results[0]["out_x"]
```

```python
import math
from contextlib import ExitStack

import concourse.bass as bass
from concourse import mybir

F32, I32, BF16 = mybir.dt.float32, mybir.dt.int32, mybir.dt.bfloat16
ALU = mybir.AluOpType
ACT = mybir.ActivationFunctionType
AX = mybir.AxisListType
ds = bass.ds

P = 128
N = 6250
E = 206250
D = 64
LAYERS = 4
AGGS = 6
DELTA = 2.5
EPS = 1e-5
TILES = -(-N // P)
TT = TILES + 1
HALF = TT // 2
DUMMY = TILES
LAST = N - (TILES - 1) * P
FC = HALF * P
VALID = ((HALF - 1) * P + LAST, (HALF - 1) * P)

BLOCK = 550
BLOCKS = E // BLOCK
SEARCHES = TILES + 1

ROUND = 64
WIN_STEP, WIN = 16, ROUND + 16
WINDOWS = E // WIN_STEP + 1
WIN_DIRECT = (E - WIN) // WIN_STEP + 1
TAIL0 = WIN_DIRECT * WIN_STEP
TAIL_REAL = E - TAIL0
TAIL = (WINDOWS - WIN_DIRECT - 1) * WIN_STEP + WIN

GROUP, SLOTS = 7, 3
BODY = GROUP * SLOTS
ITERS = -(-(ROUND + -(-E // P)) // BODY)
COLS = ITERS * BODY
FLATC = COLS + ROUND
COUNTING = max(ROUND + 2, ITERS)
BIG_TILES = -(-(E // (ROUND + 1)) // P)
BIG_GROUP = 4
BINS = ROUND + 2
BT = BINS * TILES
SCAN_CHUNKS = 7
SCAN = BT // SCAN_CHUNKS
PAY = D + 4
HUGE = 3.0e38
WIDE = 4 * P
ACT_STEPS = 3
FULL = VALID[1] // WIDE

A_AB, A_U, A_U0, A_MIX, A_BM, A_COL = 0, 128, 704, 768, 832, 896
A_ALL = A_COL + 6
NU = 3 * AGGS // 2
W_AB, W_U0, W_MIX, W_BM, W_COL, W_U = 0, 256, 384, 512, 576, 582
W_ALL = W_U + (2 * NU + 1) * D
C_BMIX, C_GT, C_BT, C_GO, C_BO, C_BU = (W_COL + i for i in range(6))
PAIRS = [(5, 0), (1, 2), (4, 3)]


def build(nc, x, src, dst, WM, bM, WU, bU, gamma_t, beta_t, Wmix, bmix, gamma_o, beta_o, out):
    assert E == BLOCKS * BLOCK and BLOCKS <= 512
    assert BT == SCAN * SCAN_CHUNKS and SCAN <= 512 and VALID[1] == FULL * WIDE
    windows = nc.dram_tensor("windows", (WINDOWS, WIN), I32).ap()
    pos_d = nc.dram_tensor("pos_d", (TILES * P, PAY), F32).ap()
    table = nc.dram_tensor("table", (TILES * P, 2 * D), F32).ap()

    with ExitStack() as ctx:
        def sb(name, shape, dt=F32):
            return ctx.enter_context(nc.sbuf_tensor(name, shape, dt))

        def sem(name):
            return ctx.enter_context(nc.semaphore(name))

        onesf = sb("onesf", [P, SCAN])
        fold = sb("fold", [P, P])
        ones_bf = sb("ones_bf", [P, P], BF16)
        below_bf = sb("below_bf", [P, P], BF16)
        prefix = sb("prefix", [64, TT])
        tiny = sb("tiny", [P, 1])
        epsc = sb("epsc", [P, 1])
        weights = sb("weights", [P, LAYERS + 1, A_ALL])
        W = sb("W", [P, W_ALL])

        flat = sb("flat", [P, 3, FLATC], I32)
        colo = sb("colo", [1, TT], I32)
        nid = sb("nid", [P, TILES], I32)
        rank_i = sb("rank_i", [P, TILES], I32)
        scal = sb("scal", [P, 8, TT])
        DEG, RDEN, HAS, AMP, ATT, TMP0, TMP1, LEN = (scal[:, k, :] for k in range(8))
        XP = sb("XP", [P, TILES, PAY])

        acc = sb("acc", [P, 2, TT, 2 * D])
        SS, MM = acc[:, 0, :, :], acc[:, 1, :, :]
        MS = sb("MS", [P, TT, 2 * D])
        B = sb("B", [P, TT, D])
        hT = sb("hT", [P, FC])
        HU = sb("HU", [P, TT, D])
        HUT = sb("HUT", [P, FC])
        rows = sb("rows", [P, BODY, 2 * D])
        idx = sb("idx", [P, BODY], I32)
        D3 = sb("D3", [P, 3 * P])
        SM = sb("SM", [P, 2 * D])
        QM = sb("QM", [P, 2 * D])
        XB = sb("XB", [P, 3 * D])
        MMH = sb("MMH", [P, 2 * D])
        VS = sb("VS", [P, 2 * D])
        negid = sb("negid", [P, P])
        ident = D3[:, 0:P]
        WS = sb("WS", [P, P])
        sums_u = sb("sums_u", [P, HALF])
        sums_o = sb("sums_o", [P, FULL + 1])
        sqs_u = sb("sqs_u", [P, HALF])
        sqs_o = sb("sqs_o", [P, FULL + 1])
        col = sb("col", [P, 16])
        Z = MS[:, :, :].rearrange("p t f -> p (t f)")[:, 0:FC]
        OT = MS[:, :, :].rearrange("p t f -> p (t f)")[:, FC:2 * FC]
        AGT = MS[:, 0:9, :].rearrange("p (c s) n -> p c (s n)", c=3)
        JUNK = HU[:, :, :].rearrange("p t f -> p (t f)")
        bank = [ctx.enter_context(nc.psum_tensor(f"bank{i}", [P, 512], F32)) for i in range(8)]

        extra = sb("extra", [1, 1], I32)
        turns = sb("turns", [1, 1], I32)
        turns_f = sb("turns_f", [1, 1])
        used_f = sb("used_f", [1, 1])
        kb = sb("kb", [P, 1])
        binsf = sb("binsf", [P, COUNTING])
        LT = sb("LT", [64, 1])
        LT2 = sb("LT2", [P, 1])

        used = [0]

        def small(n, dt=F32, rows=P):
            used[0] += n
            assert used[0] <= FC
            v = HUT[0:rows, used[0] - n:used[0]]
            return v if dt == F32 else v.bitcast(dt)
        nd = small(SEARCHES)
        ndi = small(SEARCHES, I32)
        c1 = small(SEARCHES)
        c2 = small(SEARCHES)
        blki = small(SEARCHES, I32)
        rp = small(SEARCHES)
        ndh = small(SEARCHES)
        key = small(TILES)
        binsi = small(COUNTING, I32)
        start_i = small(TILES, I32)
        win_i = small(TILES, I32)
        offb = small(4 * TILES, I32).rearrange("p (k t) -> p k t", k=4)
        body_k = small(COUNTING)
        tail_i = small(TAIL, I32, rows=1)
        flatHU = HU[:, :, :].rearrange("p t f -> p (t f)")
        big = [flatHU[:, k * WIN:(k + 1) * WIN].bitcast(I32) for k in range(2)]
        big_past = flatHU[:, 2 * WIN:2 * WIN + ROUND].bitcast(I32)
        big_keep = flatHU[:, 2 * WIN + ROUND:2 * WIN + 2 * ROUND]
        b0 = 2 * WIN + 2 * ROUND
        big_start = flatHU[:, b0:b0 + 1]
        big_len = flatHU[:, b0 + 1:b0 + 2]
        big_i, big_win = (flatHU[:, b0 + k:b0 + k + 1].bitcast(I32) for k in (2, 3))
        big_off = flatHU[:, b0 + 4:b0 + 8].bitcast(I32)
        big_idx = flatHU[:, b0 + 8:b0 + 8 + BIG_GROUP].bitcast(I32)
        flatMS = MS[:, :, :].rearrange("p t f -> p (t f)")
        samples_i = flatHU[0:1, 0:BLOCKS].bitcast(I32)
        samples = flatHU[0:1, BLOCKS:2 * BLOCKS]
        found = flatMS[:, 0:7 * BLOCK].rearrange("p (s b) -> p s b", b=BLOCK).bitcast(I32)
        junk = flatMS[:, 7 * BLOCK:7 * BLOCK + P]
        flatB = B[:, :, :].rearrange("p t f -> p (t f)")
        shrug = flatB[:, 0:10 * BLOCK // 2].bitcast(BF16).rearrange("p (s b) -> p s b", b=BLOCK)
        signs = flatB[:, 5 * BLOCK:5 * BLOCK + BLOCKS].bitcast(BF16).rearrange("p (s b) -> p s b", s=2)
        onehot = flatMS[:, 4096:4096 + BT // 2].bitcast(BF16)
        before = flatMS[:, 0:BT]
        pack = acc[:, :, :, :].rearrange("p a t f -> p (a t f)")[:, 0:TT * 3 * ROUND].bitcast(I32).rearrange("p (t w) -> p t w", w=3 * ROUND)
        past = HU[:, 0:TILES, :].bitcast(I32)
        pay = XP

        names = (
            "ld_smp ld_x ld_w tail_ld win_st dve_c pool_c places v a passed "
            "smp_done smp_ps ndh_done c1_ps c1_done c2_done "
            "hot_done ps1 ps1_used ps2 rank_done sc_pos pos_ld win_ld "
            "lenT lt_done colps big_mx big_mx2 packed flat_done turns_done "
            "h0_done h0_ps h0_ev "
            "w_now w_rest a_ps b_ps b_done tab_ready tab_first tab_sc cls "
            "kb_done big_v big_ready big_next big_found big_rows big_added big_reset "
            "idx_ready summed added "
            "b_in tile_in v_ps var_done vs_done turned agt hu_ps hut_done shift "
            "row_sum sq_done row_var fold_ps root aff1 ws_done zb_done mix_ps z_done leaky ot_done shift_o aff2 "
            "normed r_done h_next "
            "fin_ps fin_ev fin_sc").split()
        S = {n: sem(n) for n in names}
        gat = [sem(f"gathered{i}") for i in range(SLOTS)]
        blk_s = [sem(f"block_found{i}") for i in range(7)]

        def wait(eng, s, value):
            eng.wait_ge(S[s] if isinstance(s, str) else s, value)
            if not isinstance(value, int):
                eng.sem_inc(S["passed"])

        def chained(eng, name):
            n = [0]

            def step(ins):
                n[0] += 1
                ins.then_inc(S[name], 1)
                eng.wait_ge(S[name], n[0])
            return step

        block = ctx.enter_context(nc.Block())

        sums = SS[:, :, :].rearrange("p t f -> p (t f)")
        exts = MM[:, :, :].rearrange("p t f -> p (t f)")

        BIG_STEPS = 17
        STEPS_ALL = 14
        h3 = hT[:, :].rearrange("p (j n) -> p j n", n=P)
        XPx = XP[:, :, 0:D]
        (c_nmu, c_std, c_rstd, c_scale, c_bias, c_zb, c_sum, c_sq, c_about, c_off, c_slope, c_var, c_shift_u, c_shift_o,
         c_n, c_n4) = (col[:, k:k + 1] for k in range(16))
        rest = slice(VALID[1], VALID[0])
        steps = [slice(m * WIDE, min((m + 1) * WIDE, FC)) for m in range(FULL + 1)]

        def load_offsets(dve, c0):
            _, values = nc.values_load_multi_w_load_instructions(
                flat[0:1, 2, ds(c0, GROUP)], engines=[mybir.EngineType.DVE], min_val=0, max_val=DUMMY * 2 * D,
                skip_runtime_bounds_check_because="flat holds tile numbers up to DUMMY, times 2 * D")
            return values

        @block.sync
        def _(sp):
            with nc.allow_non_contiguous_dma(reason="one sample of each block"):
                sp.dma_start(samples_i[0:1, :], bass.AP(dst.tensor, 0, [[E, 1], [BLOCK, BLOCKS]])).then_inc(S["ld_smp"], 16)
            sp.wait_ge(S["dve_c"], 1)
            full = N // TILES
            sp.dma_start(pay[0:full, :, 0:D], x[0:full * TILES, :].rearrange("(p i) f -> p i f", i=TILES)).then_inc(S["ld_x"], 16)
            rest = N - full * TILES
            sp.dma_start(pay[full:full + 1, 0:rest, 0:D], x[full * TILES:N, :].rearrange("(p i) f -> p i f", p=1)).then_inc(S["ld_x"], 16)
            for h in range(2):
                r = slice(64 * h, 64 * h + 64)
                w = weights[r, 0:LAYERS, :]
                sp.dma_start(w[:, :, A_AB:A_AB + 64], WM[:, 0:64, :].rearrange("l k n -> k l n")).then_inc(S["ld_w"], 16)
                sp.dma_start(w[:, :, A_AB + 64:A_AB + 128], WM[:, 64:128, :].rearrange("l k n -> k l n")).then_inc(S["ld_w"], 16)
                sp.dma_start(w[:, :, A_U0:A_U0 + 64], WU[:, 0:64, :].rearrange("l k n -> k l n")).then_inc(S["ld_w"], 16)
                sp.dma_start(w[:, :, A_MIX:A_MIX + 64], Wmix.rearrange("l k n -> k l n")).then_inc(S["ld_w"], 16)
                for c, pair in enumerate(PAIRS):
                    for s in range(3):
                        k0 = 64 + s * AGGS * D + pair[h] * D
                        o = A_U + c * 192 + s * 64
                        sp.dma_start(w[:, :, o:o + 64], WU[:, k0:k0 + D, :].rearrange("l k n -> k l n")).then_inc(S["ld_w"], 16)
                with nc.allow_non_contiguous_dma(reason="one value per partition"):
                    for o, v in ((C_BMIX, bmix), (C_GT, gamma_t), (C_BT, beta_t), (C_GO, gamma_o), (C_BO, beta_o), (C_BU, bU)):
                        sp.dma_start(w[:, :, A_COL - W_COL + o:A_COL - W_COL + o + 1], v.rearrange("l (k n) -> k l n", n=1)).then_inc(S["ld_w"], 16)
            sp.dma_start(weights[:, 0:LAYERS, A_BM:A_BM + D], bass.AP(bM.tensor, 0, [[0, P], [D, LAYERS], [1, D]])).then_inc(S["ld_w"], 16)
            sp.wait_ge(S["c2_done"], SEARCHES)
            even = WIN_DIRECT // 16 * 16
            sp.dma_start(windows[0:even, :], bass.AP(src.tensor, 0, [[WIN_STEP, even], [1, WIN]])).then_inc(S["win_st"], 16)
            sp.dma_start(windows[even:WIN_DIRECT, :],
                         bass.AP(src.tensor, even * WIN_STEP, [[WIN_STEP, WIN_DIRECT - even], [1, WIN]])).then_inc(S["win_st"], 16)
            sp.dma_start(tail_i[0:1, 0:TAIL_REAL], src[TAIL0:E].rearrange("(p f) -> p f", p=1)).then_inc(S["tail_ld"], 16)
            sp.wait_ge(S["tail_ld"], 16)
            for i in range(WINDOWS - WIN_DIRECT):
                sp.dma_start(windows[WIN_DIRECT + i:WIN_DIRECT + i + 1, :],
                             tail_i[0:1, i * WIN_STEP:i * WIN_STEP + WIN]).then_inc(S["win_st"], 16)
            sp.wait_ge(S["tab_ready"], FULL + 1)
            sp.dma_start(table.rearrange("(p i) f -> p i f", i=TILES), MS[:, 0:TILES, :]).then_inc(S["tab_first"], 16)
            sp.wait_ge(S["sc_pos"], 16 * TILES)
            sp.dma_start(XP[:, :, :], pos_d.rearrange("(p t) f -> p t f", t=TILES)).then_inc(S["pos_ld"], 16)

            sp.wait_ge(S["fin_sc"], 16 * TILES)

        @block.scalar
        def _(act):
            def to_features(turn):
                act.wait_ge(S["h0_done"], 2 * turn + 1)
                nc.scalar.activation(c1[:, 0:TILES], c2[:, 0:TILES], ACT.Sqrt, bias=epsc[:, :], scale=1.0 / D).then_inc(S["a"], 1)
                for j in range(HALF):
                    act.wait_ge(S["h0_ps"], turn * HALF + j + 1)
                    nc.scalar.copy(hT[:, j * P:(j + 1) * P], bank[2 + j % 2][:, 0:P]).then_inc(S["h0_ev"], 1)
                    if turn == 1 and (j % 4 == 3 or j == HALF - 1):
                        act.wait_ge(S["h0_ev"], HALF + j + 1)
                        act.sem_inc(S["h_next"])

            def to_table(m, l):
                t0, n = 8 * m, min(8, TT - 8 * m)
                wait(act, "a_ps", l * (FULL + 1) + m + 1)
                a3 = bank[5 + m % 2][:, 0:n * D].rearrange("p (t f) -> p t f", f=D)
                nc.scalar.copy(MS[:, t0:t0 + n, 0:D], a3)
                nc.scalar.activation(MS[:, t0:t0 + n, D:2 * D], a3, ACT.Square).then_inc(S["tab_ready"], 1)

            act.wait_ge(S["smp_ps"], 1)
            act.wait_ge(S["ndh_done"], 1)
            for i in range(SEARCHES):
                if i >= 2:
                    act.wait_ge(S["c1_ps"], i - 1)
                nc.scalar.activation(signs[:, i % 2, :], bank[7][:, 0:BLOCKS], ACT.Sign, bias=ndh[:, i:i + 1], scale=-1.0,
                                     accum_out=c1[:, i:i + 1]).then_inc(S["c1_ps"], 1)
            to_features(0)
            for m in range(FULL + 1):
                to_table(m, 0)
            act.wait_ge(S["win_ld"], 1)
            nc.scalar.activation(TMP1, DEG, ACT.Ln, bias=onesf[:, 0:1]).then_inc(S["a"], 1)
            to_features(1)
            act.wait_ge(S["places"], 1)
            act.wait_ge(S["turns_done"], 1)
            with act.Fori(0, TILES // 7) as g:
                wait(act, "packed", g + 1)
                _, places = nc.values_load_multi_w_load_instructions(
                    colo[0:1, ds(g * 7, 7)], engines=[mybir.EngineType.Activation], min_val=0, max_val=COLS,
                    skip_runtime_bounds_check_because="colo holds numbers of columns up to COLS")
                for k in range(7):
                    t = g * 7 + k
                    wait(act, "flat_done", t + 1)
                    nc.scalar.copy(flat[:, :, ds(places[k], ROUND)],
                                   pack[:, ds(t, 1), :].rearrange("p t (k j) -> p (t k) j", k=3)).then_inc(S["flat_done"], 1)
            o = act.value_load(colo[0:1, DUMMY:TT], min_val=0, max_val=COLS)
            act.wait_ge(S["flat_done"], TILES + 1)
            nc.scalar.copy(flat[:, :, ds(o, ROUND)],
                           pack[:, DUMMY, :].rearrange("p (k j) -> p k j", k=3)).then_inc(S["flat_done"], 1)
            its = act.value_load(turns[0:1, 0:1], min_val=1, max_val=ITERS)
            with act.Fori(0, LAYERS) as l:
                with act.If(l > 0):
                    for m in range(FULL + 1):
                        to_table(m, l)

                def tile(t):
                    k = l * TILES + t
                    at = ds(t, 1)
                    flat2 = lambda v: v[:, at, :].rearrange("p t f -> p (t f)")
                    s, q, b = sums[:, ds(t * (2 * D), D)], sums[:, ds(t * (2 * D) + D, D)], flat2(B)
                    nc.scalar.mul(D3[:, P:2 * P], ident, AMP[:, at])
                    nc.scalar.mul(D3[:, 2 * P:3 * P], ident, ATT[:, at])
                    nc.scalar.mul(XB[:, 0:D], b, DEG[:, at])
                    nc.scalar.mul(XB[:, D:2 * D], b, HAS[:, at])
                    nc.scalar.mul(XB[:, 2 * D:3 * D], b, HAS[:, at]).then_inc(S["b_in"], 1)
                    end = act.value_load(colo[0:1, ds(t + 1, 1)], min_val=0, max_val=COLS)
                    wait(act, "added", l * its * BODY + end + 1)
                    nc.scalar.mul(QM[:, 0:D], q, RDEN[:, at])
                    nc.scalar.activation(QM[:, D:2 * D], s, ACT.Square, scale=RDEN[:, at])
                    nc.scalar.mul(MMH[:, :], flat2(MM), HAS[:, at])
                    nc.scalar.copy(SM[:, 0:D], s)
                    nc.scalar.mul(SM[:, D:2 * D], s, RDEN[:, at]).then_inc(S["tile_in"], 1)
                    wait(act, "v_ps", k + 1)
                    nc.scalar.activation(VS[:, 0:D], bank[0][:, 0:D], ACT.Relu).then_inc(S["var_done"], 1)
                    wait(act, "var_done", k + 1)
                    nc.scalar.activation(VS[:, D:2 * D], VS[:, 0:D], ACT.Sqrt, bias=tiny[:, :]).then_inc(S["vs_done"], 1)
                    for c in range(3):
                        wait(act, "turned", 3 * k + c + 1)
                        nc.scalar.copy(AGT[:, c, :], bank[1 + c][:, 0:3 * P]).then_inc(S["agt"], 1)

                wait(act, "b_done", (l + 1) * (FULL + 1))
                with act.Fori(0, HALF - 1) as j:
                    tile(2 * j)
                    tile(2 * j + 1)
                    wait(act, "hu_ps", l * HALF + j + 1)
                    nc.scalar.activation(HUT[:, ds(j * P, P)], bank[4][:, 0:P], ACT.Identity, bias=W[:, C_BU:C_BU + 1],
                                         accum_out=sums_u[:, ds(j, 1)]).then_inc(S["hut_done"], 1)
                    wait(act, "hut_done", l * HALF + j + 2)
                    nc.scalar.mul(c_shift_u, sums_u[:, 0:1], -1.0 / P).then_inc(S["shift"], 1)
                    wait(act, "shift", l * HALF + j + 1)
                    nc.scalar.activation(VS[:, :], HUT[:, ds(j * P, P)], ACT.Square, bias=c_shift_u,
                                         accum_out=sqs_u[:, ds(j, 1)])
                tile(TILES - 1)
                wait(act, "hu_ps", (l + 1) * HALF)
                nc.scalar.activation(HUT[:, VALID[1]:FC], bank[4][:, 0:P], ACT.Identity, bias=W[:, C_BU:C_BU + 1])
                nc.scalar.activation(OT[0:64, 0:LAST], bank[4][0:64, 0:LAST], ACT.Identity, bias=W[0:64, C_BU:C_BU + 1],
                                     accum_out=sums_u[0:64, HALF - 1:HALF]).then_inc(S["hut_done"], 1)

                nc.scalar.activation(VS[0:64, 0:LAST], bank[4][0:64, 0:LAST], ACT.Identity, bias=W[0:64, C_BU:C_BU + 1]).then_inc(S["shift"], 1)
                wait(act, "shift", (l + 1) * HALF)
                nc.scalar.activation(SM[0:64, 0:LAST], VS[0:64, 0:LAST], ACT.Square, bias=c_shift_u[0:64, :],
                                     accum_out=sqs_u[0:64, HALF - 1:HALF]).then_inc(S["sq_done"], 1)

                def root(n, scale2):
                    wait(act, "fold_ps", l * 5 + 3 * n + 2)
                    nc.scalar.activation(c_std, bank[7][:, 0:1], ACT.Sqrt, bias=epsc[:, :], scale=scale2 / N).then_inc(S["root"], 1)

                root(0, 1.0 / N)
                wait(act, "zb_done", l + 1)
                for m in range(len(steps) + 2):
                    if m < len(steps):
                        r = steps[m]
                        wait(act, "mix_ps", l * len(steps) + m + 1)
                        nc.scalar.activation(Z[:, r], bank[m % 4][:, 0:r.stop - r.start], ACT.Identity, bias=c_zb).then_inc(S["z_done"], 1)
                    if m < 2:
                        continue
                    wait(act, "ot_done", l * len(steps) + m - 1)
                    if m == 2:
                        nc.scalar.mul(c_shift_o, sums_o[:, 0:1], -1.0 / WIDE).then_inc(S["shift_o"], 1)
                        wait(act, "shift_o", l + 1)
                    h, r = (slice(0, P), steps[m - 2]) if m - 2 < FULL else (slice(0, 64), rest)
                    ins = nc.scalar.activation(JUNK[h, r], OT[h, r], ACT.Square, bias=c_shift_o[h, :], accum_out=sqs_o[h, m - 2:m - 1])
                ins.then_inc(S["sq_done"], 1)
                root(1, 1.0)
                wait(act, "aff2", l + 1)
                for r in steps[0:ACT_STEPS]:
                    nc.scalar.activation(OT[:, r], OT[:, r], ACT.Relu, bias=c_bias, scale=c_scale).then_inc(S["r_done"], 1)

        @block.gpsimd
        def _(pool):
            nc.gpsimd.iota(ndi[:, :], pattern=[[1, SEARCHES]], base=0, channel_multiplier=TILES).then_inc(S["pool_c"], 1)
            nc.gpsimd.iota(binsi[:, :], pattern=[[1, COUNTING]], base=0, channel_multiplier=0).then_inc(S["pool_c"], 1)
            pool.wait_ge(S["dve_c"], 1)
            nc.gpsimd.affine_select(out=ident, in_=onesf[:, 0:P], compare_op=ALU.is_equal, fill=0.0, base=0,
                                    pattern=[[-1, P]], channel_multiplier=1).then_inc(S["pool_c"], 1)
            nc.gpsimd.affine_select(out=junk[:, 0:P], in_=onesf[:, 0:P], compare_op=ALU.is_ge, fill=0.0, base=0,
                                    pattern=[[-1, P]], channel_multiplier=1).then_inc(S["pool_c"], 1)
            nc.gpsimd.affine_select(out=prefix[:, :], in_=onesf[0:64, 0:TT], compare_op=ALU.is_ge, fill=0.0, base=-1,
                                    pattern=[[1, TT]], channel_multiplier=-1).then_inc(S["pool_c"], 1)
            nc.gpsimd.iota(pack[:, :, 2 * ROUND:], pattern=[[2 * D, TT], [0, ROUND]], base=0, channel_multiplier=0).then_inc(S["places"], 1)
            for i in range(SEARCHES):
                if i % 10 == 0:
                    pool.wait_ge(S["c1_done"], i // 10 + 1)
                if i >= 7:
                    pool.wait_ge(S["c2_done"], i - 6)
                nc.gpsimd.indirect_dma_start(found[:, i % 7, :], None, dst.rearrange("(n b) -> n b", b=BLOCK),
                                             bass.IndirectOffsetOnAxis(ap=blki[:, i:i + 1], axis=0)).then_inc(blk_s[i % 7], 16)
            pool.wait_ge(S["rank_done"], 1)
            pool.wait_ge(S["ld_x"], 32)
            for i in range(TILES):
                nc.gpsimd.indirect_dma_start(pos_d, bass.IndirectOffsetOnAxis(ap=rank_i[:, i:i + 1], axis=0),
                                             pay[:, i, :], None).then_inc(S["sc_pos"], 16)
            pool.wait_ge(S["win_ld"], 1)
            pool.wait_ge(S["win_st"], 16 * (2 + WINDOWS - WIN_DIRECT))
            for t in range(TILES):
                nc.gpsimd.indirect_dma_start(pack[:, t, 0:WIN], None, windows,
                                             bass.IndirectOffsetOnAxis(ap=win_i[:, t:t + 1], axis=0)).then_inc(blk_s[t // 7], 16)

            pool.wait_ge(S["turns_done"], 1)
            more = pool.value_load(extra[0:1, 0:1], min_val=0, max_val=E // ROUND)
            its = pool.value_load(turns[0:1, 0:1], min_val=1, max_val=ITERS)
            pool.wait_ge(S["tab_first"], 16)
            with pool.Fori(0, LAYERS) as l:
                with pool.If(l > 0):
                    for t in range(TILES):
                        if t % 8 == 0:
                            wait(pool, "tab_ready", l * (FULL + 1) + t // 8 + 1)
                        nc.gpsimd.indirect_dma_start(table, bass.IndirectOffsetOnAxis(ap=nid[:, t:t + 1], axis=0),
                                                     MS[:, t, :], None).then_inc(S["tab_sc"], 16)
                    wait(pool, "tab_sc", l * (16 * TILES))
                with pool.If(more > 0):
                    with pool.Fori(0, more) as k:
                        with pool.Fori(0, BIG_TILES) as t:
                            n = (l * more + k) * BIG_TILES + t
                            wait(pool, "big_ready", n + 1)
                            nc.gpsimd.indirect_dma_start(big[0], None, windows,
                                                         bass.IndirectOffsetOnAxis(ap=big_win, axis=0)).then_inc(S["big_found"], 16)
                            with pool.Fori(0, ROUND // BIG_GROUP) as q:
                                wait(pool, "big_next", n * (ROUND // BIG_GROUP) + q + 1)
                                for c in range(BIG_GROUP):
                                    nc.gpsimd.indirect_dma_start(rows[:, c, :], None, table,
                                                                 bass.IndirectOffsetOnAxis(ap=big_idx[:, c:c + 1], axis=0)).then_inc(S["big_rows"], 16)
                            wait(pool, "big_added", (n + 1) * ROUND + 1)
                            nc.gpsimd.inc_swdge_sem([S["big_found"], S["big_rows"]], [16, 16 * ROUND], mode="sub")
                            pool.sem_inc(S["big_reset"])
                    pool.sem_inc(S["passed"])
                with pool.Fori(0, its) as i:
                    for b in range(SLOTS):
                        wait(pool, "idx_ready", (l * its + i) * SLOTS + b + 1)
                        for k in range(b * GROUP, (b + 1) * GROUP):
                            nc.gpsimd.indirect_dma_start(rows[:, k, :], None, table,
                                                         bass.IndirectOffsetOnAxis(ap=idx[:, k:k + 1], axis=0)).then_inc(gat[b], 16)
            for t in range(TILES):
                if t % 2 == 0:
                    pool.wait_ge(S["fin_ev"], t // 2 + 1)
                nc.gpsimd.indirect_dma_start(out, bass.IndirectOffsetOnAxis(ap=nid[:, t:t + 1], axis=0),
                                             HU[:, t, :], None, bounds_check=N - 1, oob_is_err=False).then_inc(S["fin_sc"], 16)

        @block.vector
        def _(dve):
            step = chained(dve, "v")

            def take_next_table_weights(l):
                now = weights[:, l:l + 1, :] if isinstance(l, int) else weights[:, ds(l, 1), :]
                now = now.rearrange("p l w -> p (l w)")
                for h in range(2):
                    r = slice(64 * h, 64 * h + 64)
                    nc.vector.tensor_copy(W[r, W_AB + 64 * h:W_AB + 64 * h + 64], now[r, A_AB:A_AB + D])
                    nc.vector.tensor_copy(W[r, W_AB + P + 64 * h:W_AB + P + 64 * h + 64], now[r, A_AB + D:A_AB + 2 * D])
                nc.vector.tensor_copy(W[:, W_BM:W_BM + D], now[:, A_BM:A_BM + D]).then_inc(S["w_now"], 1)

            def layer_norm(turn):
                x3 = XP[:, :, 0:D]
                h0 = B[:, 0:TILES, :]
                b3 = [P, TILES, D]
                mean, dev = c1[:, 0:TILES], c2[:, 0:TILES]
                sq3 = flatMS[:, 0:TILES * D] if turn == 0 else flatHU[:, 0:TILES * D]
                sq3 = sq3.rearrange("p (t f) -> p t f", f=D)
                step(nc.vector.tensor_reduce(mean, x3, AX.X, ALU.add))
                step(nc.vector.tensor_scalar(mean, mean, 1.0 / D, None, ALU.mult))
                if turn == 0:
                    nc.vector.memset(B[:, TILES, :], 0.0)
                else:
                    dve.wait_ge(S["h0_ev"], HALF)
                step(nc.vector.tensor_tensor(h0, x3, mean.unsqueeze(2).to_broadcast(b3), ALU.subtract))
                step(nc.vector.tensor_tensor(sq3, h0, h0, ALU.mult))
                nc.vector.tensor_reduce(dev, sq3, AX.X, ALU.add).then_inc(S["h0_done"], 1)
                dve.wait_ge(S["a"], 2 * turn + 1)
                step(nc.vector.reciprocal(rp[:, 0:TILES], mean))
                step(nc.vector.tensor_tensor(h0, h0, rp[:, 0:TILES].unsqueeze(2).to_broadcast(b3), ALU.mult))
                nc.vector.tensor_scalar(B[:, :, :], B[:, :, :], 0.0, None, ALU.max).then_inc(S["h0_done"], 1)

            nc.vector.memset(onesf[:, :], 1.0)
            nc.vector.memset(ones_bf[:, :], 1.0)
            nc.vector.memset(pay[96:128, N - TILES * (N // TILES):, :], 0.0).then_inc(S["dve_c"], 1)
            dve.wait_ge(S["ld_smp"], 16)
            nc.vector.tensor_copy(samples[0:1, :], samples_i[0:1, :]).then_inc(S["smp_done"], 1)
            dve.wait_ge(S["pool_c"], 5)
            nc.vector.tensor_copy(binsf[:, :], binsi[:, :])
            nc.vector.tensor_scalar(below_bf[:, :], junk[:, 0:P], -1.0, None, ALU.mult)
            step(nc.vector.tensor_copy(nd[:, :], ndi[:, :]))
            nc.vector.tensor_scalar(ndh[:, :], nd[:, :], -0.5, None, ALU.add).then_inc(S["ndh_done"], 1)
            nc.vector.tensor_scalar(negid[:, :], ident, -1.0, None, ALU.mult)
            nc.vector.tensor_copy(fold[:, 0:64], ident[:, 0:64])
            step(nc.vector.tensor_copy(fold[:, 64:128], ident[:, 64:128]))
            nc.vector.tensor_tensor(fold[:, 0:64], ident[:, 0:64], ident[:, 64:128], ALU.add)
            step(nc.vector.tensor_tensor(fold[:, 64:128], ident[:, 0:64], ident[:, 64:128], ALU.add))

            def pick_blocks(g):
                dve.wait_ge(S["c1_ps"], 10 * g + 10)
                r = slice(10 * g, 10 * g + 10)
                step(nc.vector.tensor_scalar(c1[:, r], c1[:, r], 0.5, 0.5 * BLOCKS - 1.0, ALU.mult, ALU.add))
                step(nc.vector.tensor_scalar(c1[:, r], c1[:, r], 0.0, None, ALU.max))
                nc.vector.tensor_copy(blki[:, r], c1[:, r]).then_inc(S["c1_done"], 1)

            pick_blocks(0)
            nc.vector.memset(tiny[:, :], 1e-30)
            nc.vector.memset(epsc[:, :], EPS)
            nc.vector.memset(tail_i[0:1, :], 0)
            nc.vector.memset(W[:, :], 0.0)
            for i in range(SEARCHES):
                if i % 10 == 1 and i + 9 < SEARCHES:
                    pick_blocks(i // 10 + 1)
                dve.wait_ge(blk_s[i % 7], 16 * (i // 7 + 1))
                if i >= 10:
                    dve.wait_ge(S["c2_done"], i - 9)
                nc.vector.tensor_scalar(shrug[:, i % 10, :], found[:, i % 7, :], nd[:, i:i + 1], 0.0,
                                        ALU.is_lt, ALU.add, accum_out=c2[:, i:i + 1]).then_inc(S["c2_done"], 1)
            dve.wait_ge(S["c2_done"], SEARCHES)
            step(nc.vector.scalar_tensor_tensor(rp[:, :], c1[:, :], float(BLOCK), c2[:, :], ALU.mult, ALU.add))
            dve.wait_ge(S["ld_x"], 32)
            payc = pay.rearrange("p t f -> p f t")
            step(nc.vector.tensor_tensor(payc[:, D + 2, :], rp[:, 1:SEARCHES], rp[:, 0:TILES], ALU.subtract))
            nc.vector.tensor_copy(payc[:, D, :], nd[:, 0:TILES])
            nc.vector.tensor_copy(payc[:, D + 1, :], rp[:, 0:TILES])
            nc.vector.memset(payc[:, D + 3, :], 0.0)
            step(nc.vector.tensor_scalar(key[:, :], payc[:, D + 2, :], float(ROUND), -1.0, ALU.min, ALU.mult))
            step(nc.vector.tensor_scalar(c1[:, 0:TILES], nd[:, 0:TILES], float(N), float(ROUND), ALU.is_ge, ALU.add))
            step(nc.vector.tensor_tensor(key[:, :], key[:, :], c1[:, 0:TILES], ALU.add))
            hot = onehot.rearrange("p (c i) -> p c i", i=TILES)
            nc.vector.tensor_tensor(hot, key[:, :].unsqueeze(1).to_broadcast([P, BINS, TILES]),
                                    binsf[:, 0:BINS].unsqueeze(2).to_broadcast([P, BINS, TILES]), ALU.is_equal).then_inc(S["hot_done"], 1)
            for k in range(SCAN_CHUNKS):
                dve.wait_ge(S["ps1"], k + 1)
                r = slice(k * SCAN, (k + 1) * SCAN)
                step(nc.vector.tensor_tensor_scan(before[:, r], onesf[:, 0:SCAN], bank[k][:, 0:SCAN],
                                                  before[:, k * SCAN - 1:k * SCAN] if k else 0.0, ALU.mult, ALU.add))
                nc.vector.nop().then_inc(S["ps1_used"], 1)
            for k in range(SCAN_CHUNKS):
                dve.wait_ge(S["ps2"], k + 1)
                r = slice(k * SCAN, (k + 1) * SCAN)
                step(nc.vector.tensor_tensor(before[:, r], before[:, r], bank[k][:, 0:SCAN], ALU.add))
            step(nc.vector.tensor_tensor(before, before, onehot, ALU.mult))
            step(nc.vector.tensor_reduce(c2[:, 0:TILES], before.rearrange("p (c i) -> p i c", i=TILES), AX.X, ALU.add))
            step(nc.vector.tensor_copy(rank_i[:, :], c2[:, 0:TILES]))
            nc.vector.tensor_scalar(start_i[:, :], rank_i[:, :], P.bit_length() - 1, None, ALU.arith_shift_right)
            step(nc.vector.tensor_scalar(win_i[:, :], rank_i[:, :], P - 1, None, ALU.bitwise_and))
            nc.vector.scalar_tensor_tensor(rank_i[:, :], win_i[:, :], float(TILES), start_i[:, :], ALU.mult, ALU.add).then_inc(S["rank_done"], 1)
            dve.wait_ge(S["ld_w"], 16 * (2 * (4 + NU + 6) + 1))
            take_next_table_weights(0)
            layer_norm(0)
            nc.vector.memset(sums_u[:, :], 0.0)
            nc.vector.memset(sums_o[:, :], 0.0)
            nc.vector.memset(sqs_u[:, :], 0.0)
            nc.vector.memset(sqs_o[:, :], 0.0)
            nc.vector.memset(col[:, 0:14], 0.0)
            for h in range(2):
                nc.vector.memset(c_n[64 * h:64 * h + 64, :], float(VALID[h]))
                nc.vector.memset(c_n4[64 * h:64 * h + 64, :], VALID[h] / 4)
            nc.vector.memset(scal[:, :, :], 0.0)
            nc.vector.memset(flat[:, 0:2, :], 0)
            nc.vector.memset(flat[:, 2, :], DUMMY * 2 * D)
            nc.vector.memset(pack[:, DUMMY, 0:2 * ROUND], 0)
            step(nc.vector.memset(weights[:, LAYERS, :], 0.0))
            nc.vector.nop().then_inc(S["flat_done"], 1)
            nc.vector.nop().then_inc(S["big_added"], 1)
            nc.vector.nop().then_inc(S["added"], 1)
            nc.vector.nop().then_inc(S["summed"], 1)
            nc.vector.nop().then_inc(S["hut_done"], 1)

            dve.wait_ge(S["pos_ld"], 16)
            XC = XP[:, :, :].rearrange("p t f -> p f t")
            nc.vector.tensor_copy(DEG[:, 0:TILES], XC[:, D + 2, :])
            step(nc.vector.tensor_copy(start_i[:, :], XC[:, D + 1, :]))
            nc.vector.tensor_scalar(LEN, DEG, float(ROUND), None, ALU.min)
            nc.vector.tensor_scalar(win_i[:, :], start_i[:, :], 4, None, ALU.arith_shift_right).then_inc(S["win_ld"], 1)
            for k in range(4):
                nc.vector.tensor_scalar(offb[:, k, :], start_i[:, :], 8 >> k, None, ALU.bitwise_and)
            nc.vector.tensor_copy(nid[:, :], XC[:, D, :])
            layer_norm(1)
            dve.wait_ge(S["lenT"], 1)
            nc.vector.tensor_reduce(LT[0:TILES, :], bank[0][0:TILES, 0:P], AX.X, ALU.max).then_inc(S["lt_done"], 1)
            nc.vector.tensor_reduce(LT2[:, :], DEG, AX.X, ALU.max).then_inc(S["big_mx"], 1)
            dve.wait_ge(S["big_mx2"], 1)
            step(nc.vector.tensor_reduce(LT2[0:1, :], bank[0][0:1, P:2 * P], AX.X, ALU.max))
            step(nc.vector.tensor_scalar(extra[0:1, :], LT2[0:1, :], -1.0, 0.0, ALU.add, ALU.max))
            step(nc.vector.tensor_scalar(extra[0:1, :], extra[0:1, :], ROUND.bit_length() - 1, None, ALU.arith_shift_right))
            dve.wait_ge(S["colps"], 1)
            nc.vector.tensor_scalar(body_k[:, :], binsf[:, :], float(BODY), None, ALU.mult)
            nc.vector.tensor_copy(colo[0:1, :], bank[1][0:1, 0:TT])
            step(nc.vector.tensor_copy(used_f[0:1, :], bank[1][0:1, TILES:TT]))
            step(nc.vector.tensor_scalar(junk[0:1, 0:COUNTING], body_k[0:1, :], used_f[0:1, :], 0.0, ALU.is_lt, ALU.add,
                                         accum_out=turns_f[0:1, :]))
            nc.vector.tensor_copy(turns[0:1, :], turns_f[0:1, :]).then_inc(S["turns_done"], 1)
            step(nc.vector.tensor_tensor(past, binsf[:, 0:ROUND].unsqueeze(1).to_broadcast([P, TILES, ROUND]),
                                         LEN[:, 0:TILES].unsqueeze(2).to_broadcast([P, TILES, ROUND]), ALU.is_ge))
            for g in range(7):
                dve.wait_ge(blk_s[g], 16 * (len(range(g, SEARCHES, 7)) + 7))
                r = slice(7 * g, 7 * g + 7)
                w = WIN
                for k in range(4):
                    s = 8 >> k
                    w -= s
                    step(nc.vector.copy_predicated(pack[:, r, 0:w], offb[:, k, r].unsqueeze(2).to_broadcast([P, 7, w]),
                                                   pack[:, r, s:s + w]))
                nc.vector.copy_predicated(pack[:, r, 1:ROUND], past[:, r, 1:], pack[:, r, 0:1].to_broadcast([P, 7, ROUND - 1]))
                step(nc.vector.tensor_scalar(pack[:, r, ROUND:2 * ROUND], past[:, r, :], -1.0, 1.0, ALU.mult, ALU.add))
                nc.vector.nop().then_inc(S["packed"], 1)
            nc.vector.tensor_scalar(HAS, DEG, 1.0, None, ALU.min)
            step(nc.vector.tensor_scalar(TMP0, DEG, 1.0, None, ALU.max))
            step(nc.vector.reciprocal(RDEN, TMP0))
            nc.vector.tensor_scalar(AMP, TMP1, 1.0 / DELTA, None, ALU.mult)
            step(nc.vector.tensor_scalar(TMP0, TMP1, 0.5, None, ALU.max))
            step(nc.vector.reciprocal(TMP0, TMP0))
            step(nc.vector.scalar_tensor_tensor(ATT, TMP0, DELTA, HAS, ALU.mult, ALU.mult))
            more = dve.value_load(extra[0:1, 0:1], min_val=0, max_val=E // ROUND)
            its = dve.value_load(turns[0:1, 0:1], min_val=1, max_val=ITERS)
            dve.wait_ge(S["flat_done"], TT + 1)
            nc.vector.tensor_copy(flat[:, 0, ds(its * BODY, BODY)], flat[:, 0, 0:BODY])
            nc.vector.tensor_copy(idx[:, :], flat[:, 0, 0:BODY]).then_inc(S["idx_ready"], SLOTS)
            def further_rounds(l):
                nc.vector.memset(kb[:, :], float(ROUND)).then_inc(S["kb_done"], 1)
                wait(dve, "kb_done", (l * (more + 1)) + 1)
                with dve.Fori(0, more) as k:
                    with dve.Fori(0, BIG_TILES) as t:
                        n = (l * more + k) * BIG_TILES + t
                        count = [0]

                        def step(ins):
                            count[0] += 1
                            ins.then_inc(S["big_v"], 1)
                            wait(dve, "big_v", n * BIG_STEPS + count[0])

                        deg = DEG[:, ds(t, 1)]
                        first = XP[:, ds(t, 1), D + 1:D + 2].rearrange("p t f -> p (t f)")
                        step(nc.vector.tensor_scalar(big_start, deg, -1.0, 0.0, ALU.add, ALU.max))
                        step(nc.vector.tensor_scalar(big_start, big_start, kb[:, :], None, ALU.min))
                        step(nc.vector.tensor_tensor(big_start, big_start, first, ALU.add))
                        step(nc.vector.tensor_scalar(big_len, deg, kb[:, :], None, ALU.subtract))
                        step(nc.vector.tensor_copy(big_i, big_start))
                        for b in range(4):
                            nc.vector.tensor_scalar(big_off[:, b:b + 1], big_i, 8 >> b, None, ALU.bitwise_and)
                        nc.vector.tensor_scalar(big_past, binsf[:, 0:ROUND], big_len, None, ALU.is_ge)
                        step(nc.vector.tensor_scalar(big_win, big_i, 4, None, ALU.arith_shift_right))
                        step(nc.vector.tensor_scalar(big_keep, big_past, -1.0, 1.0, ALU.mult, ALU.add))
                        nc.vector.nop().then_inc(S["big_ready"], 1)
                        dve.wait_ge(S["big_found"], 16)
                        cur, nxt, w = *big, WIN
                        for b in range(4):
                            s = 8 >> b
                            w -= s
                            step(nc.vector.tensor_copy(nxt[:, 0:w], cur[:, 0:w]))
                            step(nc.vector.copy_predicated(nxt[:, 0:w], big_off[:, b:b + 1].to_broadcast([P, w]), cur[:, s:s + w]))
                            cur, nxt = nxt, cur
                        step(nc.vector.tensor_copy(nxt[:, 0:ROUND], cur[:, 0:ROUND]))
                        step(nc.vector.copy_predicated(nxt[:, 0:ROUND], big_past, cur[:, 0:1].to_broadcast([P, ROUND])))
                        assert count[0] == BIG_STEPS, count[0]
                        with dve.Fori(0, ROUND // BIG_GROUP) as q:
                            m = n * (ROUND // BIG_GROUP) + q
                            nc.vector.tensor_copy(big_idx, nxt[:, ds(q * BIG_GROUP, BIG_GROUP)]).then_inc(S["big_next"], 1)
                            wait(dve, "big_rows", q * (16 * BIG_GROUP) + 16 * BIG_GROUP)
                            for c in range(BIG_GROUP):
                                row = rows[:, c, :]
                                wait(dve, "big_added", m * BIG_GROUP + c + 1)
                                nc.vector.scalar_tensor_tensor(sums[:, ds(t * (2 * D), 2 * D)], row, big_keep[:, ds(q * BIG_GROUP + c, 1)],
                                                               sums[:, ds(t * (2 * D), 2 * D)], ALU.mult, ALU.add)
                                nc.vector.tensor_tensor(exts[:, ds(t * (2 * D), D)], exts[:, ds(t * (2 * D), D)], row[:, 0:D], ALU.max)
                                nc.vector.tensor_tensor(exts[:, ds(t * (2 * D) + D, D)], exts[:, ds(t * (2 * D) + D, D)], row[:, 0:D],
                                                        ALU.min).then_inc(S["big_added"], 1)
                        wait(dve, "big_reset", n + 1)
                    nc.vector.tensor_scalar(kb[:, :], kb[:, :], float(ROUND), None, ALU.add).then_inc(S["kb_done"], 1)
                    wait(dve, "kb_done", l * (more + 1) + k + 2)
                wait(dve, "big_added", (l * more + more) * (BIG_TILES * ROUND) + 1)

            with dve.Fori(0, LAYERS) as l:
                n_step = [0]

                def step(ins):
                    n_step[0] += 1
                    ins.then_inc(S["cls"], 1)
                    wait(dve, "cls", l * STEPS_ALL + n_step[0])

                for m in range(FULL + 1):
                    t0, n = 8 * m, min(8, TT - 8 * m)
                    wait(dve, "b_ps", l * (FULL + 1) + m + 1)
                    nc.vector.tensor_tensor(B[:, t0:t0 + n, :], bank[1 + m % 2][:, 0:n * D].rearrange("p (t f) -> p t f", f=D),
                                            W[:, W_BM:W_BM + D].unsqueeze(1).to_broadcast([P, n, D]), ALU.add).then_inc(S["b_done"], 1)
                now = weights[:, ds(l, 1), :].rearrange("p l w -> p (l w)")
                for h in range(2):
                    r = slice(64 * h, 64 * h + 64)
                    nc.vector.tensor_copy(W[r, W_U0 + 64 * h:W_U0 + 64 * h + 64], now[r, A_U0:A_U0 + D])
                    nc.vector.tensor_copy(W[r, W_MIX + 64 * h:W_MIX + 64 * h + 64], now[r, A_MIX:A_MIX + D])
                nc.vector.tensor_copy(W[:, W_U:W_U + 2 * NU * D].rearrange("p (i z f) -> p i z f", z=2, f=D)[:, :, 1, :],
                                      now[:, A_U:A_U + NU * D].rearrange("p (i f) -> p i f", f=D))
                nc.vector.tensor_copy(W[:, W_COL:W_U], now[:, A_COL:A_ALL]).then_inc(S["w_rest"], 1)
                wait(dve, "b_done", (l + 1) * (FULL + 1))
                take_next_table_weights(l + 1)
                nc.vector.memset(SS[:, :, :], 0.0)
                nc.vector.memset(MM[:, :, 0:D], -HUGE)
                step(nc.vector.memset(MM[:, :, D:2 * D], HUGE))
                with dve.If(more > 0):
                    further_rounds(l)
                with dve.Fori(0, its) as i:
                    for b in range(SLOTS):
                        c0 = i * BODY + b * GROUP
                        wait(dve, gat[b], (l * its + i) * (16 * GROUP) + 16 * GROUP)
                        offs = load_offsets(dve, c0)
                        for k in range(GROUP):
                            row, o = rows[:, b * GROUP + k, :], offs[k]
                            n = l * its * BODY + c0 + k + 1
                            dve.wait_ge(S["summed"], n)
                            nc.vector.scalar_tensor_tensor(sums[:, ds(o, 2 * D)], row, flat[:, 1, ds(c0 + k, 1)],
                                                           sums[:, ds(o, 2 * D)], ALU.mult, ALU.add).then_inc(S["summed"], 1)
                            dve.wait_ge(S["added"], n)
                            nc.vector.tensor_tensor(exts[:, ds(o, D)], exts[:, ds(o, D)], row[:, 0:D], ALU.max)
                            nc.vector.tensor_tensor(exts[:, ds(o + D, D)], exts[:, ds(o + D, D)], row[:, 0:D],
                                                    ALU.min).then_inc(S["added"], 1)
                        nc.vector.tensor_copy(idx[:, b * GROUP:(b + 1) * GROUP],
                                              flat[:, 0, ds(c0 + BODY, GROUP)]).then_inc(S["idx_ready"], 1)

                def norm(n, sums_n, sqs_n, c_shift, scale2, gam, bet):
                    step(nc.vector.tensor_reduce(c_sum, sums_n, AX.X, ALU.add))
                    dve.sem_inc(S["row_sum"])
                    wait(dve, "sq_done", l * 2 + n + 1)
                    nc.vector.scalar_tensor_tensor(c_about, c_shift, c_n, c_sum, ALU.mult, ALU.add)
                    nc.vector.tensor_reduce(c_sq, sqs_n, AX.X, ALU.add)
                    wait(dve, "fold_ps", l * 5 + 3 * n + 1)
                    step(nc.vector.tensor_scalar(c_nmu, bank[7][:, 0:1], -1.0 / N, None, ALU.mult))
                    step(nc.vector.tensor_scalar(c_off, c_nmu, c_shift, 2.0, ALU.subtract, ALU.mult))
                    step(nc.vector.scalar_tensor_tensor(c_slope, c_off, c_n4, c_about, ALU.mult, ALU.add))
                    nc.vector.scalar_tensor_tensor(c_var, c_slope, c_off, c_sq, ALU.mult, ALU.add).then_inc(S["row_var"], 1)
                    wait(dve, "root", l * 2 + n + 1)
                    step(nc.vector.reciprocal(c_rstd, c_std))
                    step(nc.vector.tensor_scalar(c_scale, c_rstd, W[:, gam:gam + 1], math.sqrt(scale2), ALU.mult, ALU.mult))
                    return nc.vector.scalar_tensor_tensor(c_bias, c_nmu, c_scale, W[:, bet:bet + 1], ALU.mult, ALU.add)

                wait(dve, "hut_done", (l + 1) * HALF + 1)
                norm(0, sums_u[:, :], sqs_u[:, :], c_shift_u, 1.0 / N, C_GT, C_BT).then_inc(S["aff1"], 1)
                nc.vector.tensor_scalar(WS[:, :], W[:, W_MIX:W_MIX + P], c_scale, None, ALU.mult).then_inc(S["ws_done"], 1)
                wait(dve, "fold_ps", l * 5 + 3)
                nc.vector.tensor_tensor(c_zb, bank[7][:, 0:1], W[:, C_BMIX:C_BMIX + 1], ALU.add).then_inc(S["zb_done"], 1)
                for m in range(len(steps) + 1):
                    if m < len(steps):
                        r = steps[m]
                        wait(dve, "z_done", l * len(steps) + m + 1)
                        nc.vector.scalar_tensor_tensor(Z[:, r], Z[:, r], 0.01, Z[:, r], ALU.mult, ALU.max).then_inc(S["leaky"], 1)
                    if m == 0:
                        continue
                    r = steps[m - 1]
                    wait(dve, "leaky", l * len(steps) + m)
                    if m - 1 < FULL:
                        nc.vector.scalar_tensor_tensor(OT[:, r], Z[:, r], 1.0, hT[:, r], ALU.mult, ALU.add,
                                                       accum_out=sums_o[:, m - 1:m]).then_inc(S["ot_done"], 1)
                    else:
                        step(nc.vector.tensor_tensor(OT[:, r], Z[:, r], hT[:, r], ALU.add))
                        ins = nc.vector.tensor_reduce(sums_o[0:64, m - 1:m], OT[0:64, rest], AX.X, ALU.add).then_inc(S["ot_done"], 1)
                wait(dve, "ot_done", (l + 1) * len(steps))
                norm(1, sums_o[:, :], sqs_o[:, :], c_shift_o, 1.0, C_GO, C_BO).then_inc(S["aff2"], 1)
                wait(dve, "aff2", l + 1)
                for m in range(len(steps)):
                    k = m + ACT_STEPS
                    if k < len(steps):
                        nc.vector.tensor_scalar(OT[:, steps[k]], OT[:, steps[k]], c_scale, c_bias, ALU.mult, ALU.add).then_inc(S["normed"], 1)
                    r = steps[m]
                    if m < ACT_STEPS:
                        wait(dve, "r_done", l * ACT_STEPS + m + 1)
                        nc.vector.tensor_tensor(hT[:, r], OT[:, r], hT[:, r], ALU.add).then_inc(S["h_next"], 1)
                    else:
                        wait(dve, "normed", l * (len(steps) - ACT_STEPS) + m - ACT_STEPS + 1)
                        nc.vector.scalar_tensor_tensor(hT[:, r], OT[:, r], 0.0, hT[:, r], ALU.max, ALU.add).then_inc(S["h_next"], 1)
                assert n_step[0] == STEPS_ALL, n_step[0]
            for j in range(HALF):
                dve.wait_ge(S["fin_ps"], j + 1)
                n = min(2, TILES - 2 * j)
                nc.vector.tensor_tensor(HU[:, 2 * j:2 * j + n, :], bank[j % 2][:, 0:n * D].rearrange("p (a f) -> p a f", a=n),
                                        XPx[:, 2 * j:2 * j + n, :], ALU.add).then_inc(S["fin_ev"], 1)

        @block.tensor
        def _(pe):
            def to_features(turn):
                pe.wait_ge(S["h0_done"], 2 * turn + 2)
                for j in range(HALF):
                    if turn or j >= 2:
                        pe.wait_ge(S["h0_ev"], turn * HALF + j - 1)
                    nc.tensor.transpose(bank[2 + j % 2][:, 0:P], B[:, 2 * j:2 * j + 2, :], ident).then_inc(S["h0_ps"], 1)

            def project(m, out_bank, w, done):
                r = steps[m]
                for j in range(r.start // P, r.stop // P):
                    o = (j % 4) * P
                    ins = nc.tensor.matmul(bank[out_bank + m % 2][:, o:o + P], h3[:, j, :], W[:, w:w + P], start=True, stop=True)
                ins.then_inc(S[done], 1)

            pe.wait_ge(S["smp_done"], 1)
            pe.wait_ge(S["dve_c"], 1)
            nc.tensor.matmul(bank[7][:, 0:BLOCKS], onesf[0:1, 0:P], samples[0:1, :], start=True, stop=True).then_inc(S["smp_ps"], 1)
            pe.wait_ge(S["hot_done"], 1)
            for k in range(SCAN_CHUNKS):
                nc.tensor.matmul(bank[k][:, 0:SCAN], ones_bf[:, :], onehot[:, k * SCAN:(k + 1) * SCAN],
                                 start=True, stop=True).then_inc(S["ps1"], 1)
            for k in range(SCAN_CHUNKS):
                pe.wait_ge(S["ps1_used"], k + 1)
                nc.tensor.matmul(bank[k][:, 0:SCAN], below_bf[:, :], onehot[:, k * SCAN:(k + 1) * SCAN],
                                 start=True, stop=True).then_inc(S["ps2"], 1)
            to_features(0)
            for m, r in enumerate(steps):
                pe.wait_ge(S["h0_ev"], r.stop // P)
                if m >= 2:
                    pe.wait_ge(S["tab_ready"], m - 1)
                project(m, 5, W_AB, "a_ps")
            pe.wait_ge(S["win_ld"], 1)
            nc.tensor.transpose(bank[0][0:TILES, 0:P], LEN[:, 0:TILES], ident).then_inc(S["lenT"], 1)
            pe.wait_ge(S["lt_done"], 1)
            nc.tensor.matmul(bank[1][0:1, 0:TT], LT[0:TILES, :], prefix[0:TILES, :], start=True, stop=True).then_inc(S["colps"], 1)
            pe.wait_ge(S["big_mx"], 1)
            nc.tensor.transpose(bank[0][0:1, P:2 * P], LT2[:, :], ident).then_inc(S["big_mx2"], 1)
            to_features(1)
            pe.wait_ge(S["turns_done"], 1)
            pe.wait_ge(S["h0_ev"], 2 * HALF)
            with pe.Fori(0, LAYERS) as l:

                wait(pe, "w_now", l + 1)
                with pe.If(l > 0):
                    for m in range(FULL + 1):
                        wait(pe, "h_next", l * len(steps) + m + 1)
                        if m >= 2:
                            wait(pe, "tab_ready", l * (FULL + 1) + m - 1)
                        project(m, 5, W_AB, "a_ps")
                for m in range(FULL + 1):
                    wait(pe, "h_next", l * len(steps) + m + 1)
                    if m >= 2:
                        wait(pe, "b_done", l * (FULL + 1) + m - 1)
                    project(m, 1, W_AB + P, "b_ps")
                wait(pe, "b_done", (l + 1) * (FULL + 1))
                wait(pe, "w_rest", l + 1)

                def tile(t, half, last):
                    k = l * TILES + t
                    wait(pe, "b_in", k + 1)
                    nc.tensor.matmul(bank[1][:, 0:3 * P], XB[:, 0:2 * D], D3[:, :], start=True, stop=False)
                    nc.tensor.matmul(bank[2][:, 0:3 * P], XB[:, D:3 * D], D3[:, :], start=True, stop=False)
                    wait(pe, "tile_in", k + 1)
                    nc.tensor.matmul(bank[0][:, 0:D], ident, QM[:, 0:D], start=True, stop=False)
                    nc.tensor.matmul(bank[0][:, 0:D], negid[:, :], QM[:, D:2 * D], start=False, stop=True).then_inc(S["v_ps"], 1)
                    nc.tensor.matmul(bank[1][:, 0:3 * P], SM[:, :], D3[:, :], start=False, stop=True).then_inc(S["turned"], 1)
                    nc.tensor.matmul(bank[2][:, 0:3 * P], MMH[:, :], D3[:, :], start=False, stop=True).then_inc(S["turned"], 1)
                    wait(pe, "vs_done", k + 1)
                    nc.tensor.matmul(bank[3][:, 0:3 * P], VS[:, :], D3[:, :], start=True, stop=True).then_inc(S["turned"], 1)
                    for c in range(3):
                        wait(pe, "agt", 3 * k + c + 1)
                        for i in range(3):
                            w = W_U + (2 * (3 * c + i) + (1 - half)) * D
                            ins = nc.tensor.matmul(bank[4][:, 0:P], W[:, w:w + P], AGT[:, c, i * P:(i + 1) * P],
                                                   start=False, stop=last and c == 2 and i == 2)
                    if last:
                        ins.then_inc(S["hu_ps"], 1)

                def own(j):
                    nc.tensor.matmul(bank[4][:, 0:P], W[:, W_U0:W_U0 + P], hT[:, ds(j * P, P)], start=True, stop=False)

                with pe.Fori(0, HALF - 1) as j:
                    wait(pe, "hut_done", l * HALF + j + 1)
                    own(j)
                    tile(2 * j, 0, False)
                    tile(2 * j + 1, 1, True)
                wait(pe, "hut_done", (l + 1) * HALF)
                own(HALF - 1)
                tile(TILES - 1, 0, True)

                def fold_rows(value, ready, count):
                    wait(pe, ready, count)
                    nc.tensor.matmul(bank[7][:, 0:1], fold[:, :], value, start=True, stop=True).then_inc(S["fold_ps"], 1)
                fold_rows(c_sum, "row_sum", l * 2 + 1)
                fold_rows(c_var, "row_var", l * 2 + 1)
                wait(pe, "aff1", l + 1)
                nc.tensor.matmul(bank[7][:, 0:1], W[:, W_MIX:W_MIX + P], c_bias, start=True, stop=True).then_inc(S["fold_ps"], 1)
                wait(pe, "ws_done", l + 1)
                for m, r in enumerate(steps):
                    if m >= 4:
                        wait(pe, "z_done", l * len(steps) + m - 3)
                    nc.tensor.matmul(bank[m % 4][:, 0:r.stop - r.start], WS[:, :], HUT[:, r], start=True, stop=True).then_inc(S["mix_ps"], 1)
                fold_rows(c_sum, "row_sum", l * 2 + 2)
                fold_rows(c_var, "row_var", l * 2 + 2)
            pe.wait_ge(S["h_next"], (LAYERS + 1) * (FULL + 1))
            for j in range(HALF):
                if j >= 2:
                    pe.wait_ge(S["fin_ev"], j - 1)
                nc.tensor.transpose(bank[j % 2][:, 0:P], h3[:, j, :], ident).then_inc(S["fin_ps"], 1)


_INS = ["x", "src", "dst", "WM", "bM", "WU", "bU", "gamma_t", "beta_t", "Wmix", "bmix", "gamma_o", "beta_o"]


def kernel(**inputs):
    import numpy as np
    import concourse.bacc as bacc
    from concourse.bass_utils import run_bass_kernel_spmd

    nc = bacc.Bacc("TRN2", target_bir_lowering=False, num_devices=1)
    arrays, args = {}, []
    for name in _INS:
        a = np.ascontiguousarray(inputs[name if name in ("x", "src", "dst") else "L0_gnn_" + name])
        arrays[f"in_{name}"] = a
        args.append(nc.dram_tensor(f"in_{name}", a.shape, mybir.dt.from_np(a.dtype), kind="ExternalInput").ap())
    out = nc.dram_tensor("out_x", (N, D), F32, kind="ExternalOutput").ap()
    build(nc, *args, out)
    r = run_bass_kernel_spmd(nc, [arrays], core_ids=[0])
    return r.results[0]["out_x"]
```
